# Optimizing a Trainium2 kernel written in Bass

```python
import numpy as np
import jax
import jax.numpy as jnp

def _softmax(x, axis=-1):
    return jax.nn.softmax(x, axis=axis)

def _gelu(x):
    return jax.nn.gelu(x, approximate=True)

def _silu(x):
    return jax.nn.silu(x)

def _sigmoid(x):
    return jax.nn.sigmoid(x)

def _layernorm(x, axis=-1, eps=1e-05):
    m = jnp.mean(x, axis=axis, keepdims=True)
    v = jnp.var(x, axis=axis, keepdims=True)
    return (x - m) / jnp.sqrt(v + eps)

def _scatter_add(tgt, idx, src, axis=0):
    return tgt.at[idx].add(src)

def _segment_sum(src, seg, n):
    return jax.ops.segment_sum(src, seg, n)
kernel_name = 'mk_xattn_ffn_d1_seqx_r8_1c531d'

def setup_inputs(seed: int=0):
    np.random.seed(seed)
    _w = jnp.asarray

    def _rec_inputs():
        import jax
        import jax.numpy as jnp
        _rk = jax.random.key(seed)
        x = -0.0002928 + 1 * jax.random.normal(jax.random.fold_in(_rk, 1), (32, 128, 128), jnp.float32)
        _lenS = 128 - jax.random.randint(jax.random.fold_in(_rk, 7), (32,), 0, max(1, 128 // 4) + 1, jnp.int32)
        _lenS2 = 128 - jax.random.randint(jax.random.fold_in(_rk, 8), (32,), 0, max(1, 128 // 4) + 1, jnp.int32)
        _ctx_1024P = jax.random.normal(jax.random.fold_in(_rk, 11), (32, 16, 128), jnp.float32)
        _ctx_1024c = jax.random.dirichlet(jax.random.fold_in(_rk, 511), 0.3 * jnp.ones((16,), jnp.float32), (32, 128))
        _ctx_1024t = jnp.einsum('bsk,bkd->bsd', _ctx_1024c, _ctx_1024P)
        _ctx_1024t = _ctx_1024t * jax.lax.rsqrt(jnp.mean(jnp.square(_ctx_1024t)) + 1e-12) * 0.953939
        ctx_1024 = -1.39393e-06 + 0.999914 * (_ctx_1024t + 0.3 * jax.random.normal(jax.random.fold_in(_rk, 611), (32, 128, 128), jnp.float32))
        return (x, ctx_1024)
    x, ctx_1024 = _rec_inputs()

    def _L0_xattn_setup():
        import jax, jax.numpy as jnp
        import numpy as np
        import math
        HIDDEN = 128
        HEADS = 16
        HEAD = HIDDEN // HEADS
        SCALE_BASE = 512.0

        def _gammas(heads):
            return 1.0 - jnp.exp(jnp.linspace(math.log(1.0 / 32.0), math.log(1.0 / 512.0), heads))

        def _xpos(x, downscale):
            S, d = (x.shape[2], x.shape[3])
            half = d // 2
            base_scale = (jnp.arange(0, d, 2, dtype=jnp.float32) + 0.4 * d) / (1.4 * d)
            pos = jnp.arange(S, dtype=jnp.float32)
            scale = base_scale[None, :] ** (pos / SCALE_BASE)[:, None]
            if downscale:
                scale = 1.0 / scale
            inv_freq = 1.0 / 10000.0 ** (jnp.arange(half, dtype=jnp.float32) / half)
            sinusoid = pos[:, None] * inv_freq[None, :]
            sin = jnp.repeat(jnp.sin(sinusoid) * scale, 2, axis=-1)
            cos = jnp.repeat(jnp.cos(sinusoid) * scale, 2, axis=-1)
            x1 = x[..., ::2]
            x2 = x[..., 1::2]
            rot = jnp.stack([-x2, x1], axis=-1).reshape(x.shape)
            return x * cos + rot * sin

        def _decay_mask(S, gammas):
            n = jnp.arange(S)[:, None]
            m = jnp.arange(S)[None, :]
            diff = (n - m).astype(jnp.float32)
            mask = n >= m
            pw = jnp.maximum(diff, 0.0)[None, :, :]
            return jnp.where(mask[None, :, :], gammas[:, None, None] ** pw, 0.0)

        def retention_forward(Q, K, V):
            B, S, _ = Q.shape

            def split(x, hd):
                return x.reshape(B, S, HEADS, hd).transpose(0, 2, 1, 3)
            q = _xpos(split(Q, HEAD), downscale=False)
            k = _xpos(split(K, HEAD), downscale=True)
            v = split(V, HEAD)
            D = _decay_mask(S, _gammas(HEADS).astype(Q.dtype))
            scores = jnp.einsum('bhsd,bhtd->bhst', q, k) * D[None]
            out = jnp.einsum('bhst,bhtd->bhsd', scores, v)
            return out.transpose(0, 2, 1, 3).reshape(B, S, HEADS * HEAD)
        key = jax.random.key(seed)
        kq, kk, kv = jax.random.split(key, 3)
        B, S = (2, 256)
        return {'Q': jax.random.normal(kq, (B, S, HIDDEN), dtype=jnp.float32), 'K': jax.random.normal(kk, (B, S, HIDDEN), dtype=jnp.float32), 'V': jax.random.normal(kv, (B, S, HIDDEN), dtype=jnp.float32)}
    _L0_xattn_all = _L0_xattn_setup()
    _L0_xattn_in = {k: v for k, v in _L0_xattn_all.items() if k in ()}
    del _L0_xattn_all

    def _L0_ffn_setup():
        import jax, jax.numpy as jnp
        import numpy as np
        TOPK = 2
        EPS = 1e-06
        key = jax.random.key(seed)
        ks = jax.random.split(key, 8)
        b, t, d, h, n = (2, 128, 128, 256, 16)
        x = jax.random.normal(ks[0], (b, t, d), dtype=jnp.float32)
        router_w = jax.random.normal(ks[1], (n, d), dtype=jnp.float32) * (1.0 / np.sqrt(d))
        router_bias = jnp.zeros((n,), dtype=jnp.float32)
        bank_mag = jax.random.normal(ks[2], (n, d, h), dtype=jnp.float32) * (1.0 / np.sqrt(d))
        bank_freq = jax.random.uniform(ks[3], (n, d, h), dtype=jnp.float32, minval=0.5, maxval=2.0) * (1.0 / np.sqrt(d))
        bank_phase = jax.random.uniform(ks[4], (n, h), dtype=jnp.float32, minval=-0.3, maxval=0.3)
        bank_down = jax.random.normal(ks[5], (n, h, d), dtype=jnp.float32) * (1.0 / np.sqrt(h))
        norm_w = jnp.ones((d,), dtype=jnp.float32)
        return {'x': x, 'router_w': router_w, 'router_bias': router_bias, 'bank_mag': bank_mag, 'bank_freq': bank_freq, 'bank_phase': bank_phase, 'bank_down': bank_down, 'norm_w': norm_w}
    _L0_ffn_all = _L0_ffn_setup()
    _L0_ffn_in = {k: v for k, v in _L0_ffn_all.items() if k in ('router_w', 'router_bias', 'bank_mag', 'bank_freq', 'bank_phase', 'bank_down', 'norm_w')}
    del _L0_ffn_all
    return {'x': x, 'ctx_1024': ctx_1024, 'L0_ffn_router_w': _L0_ffn_in['router_w'], 'L0_ffn_router_bias': _L0_ffn_in['router_bias'], 'L0_ffn_bank_mag': _L0_ffn_in['bank_mag'], 'L0_ffn_bank_freq': _L0_ffn_in['bank_freq'], 'L0_ffn_bank_phase': _L0_ffn_in['bank_phase'], 'L0_ffn_bank_down': _L0_ffn_in['bank_down'], 'L0_ffn_norm_w': _L0_ffn_in['norm_w']}

def reference(x, ctx_1024, L0_ffn_router_w, L0_ffn_router_bias, L0_ffn_bank_mag, L0_ffn_bank_freq, L0_ffn_bank_phase, L0_ffn_bank_down, L0_ffn_norm_w):
    import jax
    import jax.numpy as jnp

    def _L0_xattn_ref(Q, K, V):
        import jax, jax.numpy as jnp
        import numpy as np
        import math
        HIDDEN = 128
        HEADS = 16
        HEAD = HIDDEN // HEADS
        SCALE_BASE = 512.0

        def _gammas(heads):
            return 1.0 - jnp.exp(jnp.linspace(math.log(1.0 / 32.0), math.log(1.0 / 512.0), heads))

        def _xpos(x, downscale):
            S, d = (x.shape[2], x.shape[3])
            half = d // 2
            base_scale = (jnp.arange(0, d, 2, dtype=jnp.float32) + 0.4 * d) / (1.4 * d)
            pos = jnp.arange(S, dtype=jnp.float32)
            scale = base_scale[None, :] ** (pos / SCALE_BASE)[:, None]
            if downscale:
                scale = 1.0 / scale
            inv_freq = 1.0 / 10000.0 ** (jnp.arange(half, dtype=jnp.float32) / half)
            sinusoid = pos[:, None] * inv_freq[None, :]
            sin = jnp.repeat(jnp.sin(sinusoid) * scale, 2, axis=-1)
            cos = jnp.repeat(jnp.cos(sinusoid) * scale, 2, axis=-1)
            x1 = x[..., ::2]
            x2 = x[..., 1::2]
            rot = jnp.stack([-x2, x1], axis=-1).reshape(x.shape)
            return x * cos + rot * sin

        def _decay_mask(S, gammas):
            n = jnp.arange(S)[:, None]
            m = jnp.arange(S)[None, :]
            diff = (n - m).astype(jnp.float32)
            mask = n >= m
            pw = jnp.maximum(diff, 0.0)[None, :, :]
            return jnp.where(mask[None, :, :], gammas[:, None, None] ** pw, 0.0)

        def retention_forward(Q, K, V):
            B, S, _ = Q.shape

            def split(x, hd):
                return x.reshape(B, S, HEADS, hd).transpose(0, 2, 1, 3)
            q = _xpos(split(Q, HEAD), downscale=False)
            k = _xpos(split(K, HEAD), downscale=True)
            v = split(V, HEAD)
            D = _decay_mask(S, _gammas(HEADS).astype(Q.dtype))
            scores = jnp.einsum('bhsd,bhtd->bhst', q, k) * D[None]
            out = jnp.einsum('bhst,bhtd->bhsd', scores, v)
            return out.transpose(0, 2, 1, 3).reshape(B, S, HEADS * HEAD)
        return retention_forward(Q, K, V)

    def _L0_ffn_ref(x, router_w, router_bias, bank_mag, bank_freq, bank_phase, bank_down, norm_w):
        import jax, jax.numpy as jnp
        import numpy as np
        TOPK = 2
        EPS = 1e-06
        b, t, d = x.shape
        scores = jnp.einsum('btd,nd->btn', x, router_w) + router_bias
        topv, topi = jax.lax.top_k(scores, TOPK)
        weights = jax.nn.softmax(topv, axis=-1)
        fx = x.reshape(b * t, d)
        mag = jnp.einsum('td,ndh->tnh', fx, bank_mag)
        freq = jnp.einsum('td,ndh->tnh', fx, bank_freq)
        hidden = jnp.tanh(mag) * jnp.cos(jax.nn.softplus(freq) + 0.1 + bank_phase[None, :, :])
        out_all = jnp.einsum('tnh,nhd->tnd', hidden, bank_down)
        ti = topi.reshape(b * t, TOPK)
        sel = jnp.take_along_axis(out_all, ti[:, :, None], axis=1)
        out = jnp.einsum('tkd,tk->td', sel, weights.reshape(b * t, TOPK)).reshape(b, t, d)
        out = out * jax.lax.rsqrt(jnp.mean(out * out, axis=-1, keepdims=True) + EPS) * norm_w
        return out
    x = x + _L0_xattn_ref(_layernorm(x, axis=-1), ctx_1024, ctx_1024)
    x = x + _L0_ffn_ref(_layernorm(x, axis=-1), L0_ffn_router_w, L0_ffn_router_bias, L0_ffn_bank_mag, L0_ffn_bank_freq, L0_ffn_bank_phase, L0_ffn_bank_down, L0_ffn_norm_w)
    return x

_drawn_inputs = setup_inputs


def setup_inputs(seed=0):
    import zlib

    import numpy as np

    out = dict(_drawn_inputs(seed))
    spreads = {'L0_ffn_router_bias': (0.0, 0.8), 'L0_ffn_norm_w': (1.0, 0.6)}
    factors = {'L0_ffn_router_w': 3.021,
     'L0_ffn_bank_mag': 2.84,
     'L0_ffn_bank_freq': 8.0,
     'L0_ffn_bank_phase': 8.0,
     'L0_ffn_bank_down': 2.848}
    for name, (base, spread) in spreads.items():
        noise = np.random.default_rng([zlib.crc32(name.encode()), seed]).standard_normal(out[name].shape)
        drawn = base * np.exp(spread * noise) if base else spread * noise
        out[name] = jnp.asarray(drawn.astype(out[name].dtype))
    for name, factor in factors.items():
        out[name] = (out[name] * factor).astype(out[name].dtype)
    return out
```

```python
from contextlib import ExitStack

import numpy as np

import concourse.bass as bass
from concourse import mybir

F32 = mybir.dt.float32
BF16 = mybir.dt.bfloat16
I32 = mybir.dt.int32
U32 = mybir.dt.uint32
ALU = mybir.AluOpType
ACT = mybir.ActivationFunctionType
AX = mybir.AxisListType

P = 128
B = 32
HEADS = 16
HEAD = P // HEADS
JH = 4
GRP = 4
NG = B // GRP
E = 16
H = 256
K = 2
TOK = B * P
ROW = 132
REG = TOK + P
NULL_ROW = E * REG
NT = TOK * K // P + E
TG = 8
PAIRS = TG // 2
NTG = NT // TG
ZEROED = 8
DROP = 1 << 20
LN_EPS, RMS_EPS = 1e-5, 1e-6
TWO_PI = 2 * np.pi
MAGIC = 1.5 * 2.0 ** 23

C_CQ, C_SQ, C_CK, C_SK, C_CAUSAL, C_IDENT, C_BEFORE, C_ONES = (P * i for i in range(8))
C_IOTA = 8 * P
C_BASE = C_IOTA + E
C_TILE = C_BASE + E
C_END = C_TILE + NT


def constants():
    c = np.zeros((P, C_END), np.float64)
    pos = np.arange(P)[:, None]
    f = np.arange(P)[None, :]
    head, pair, odd = f // HEAD, (f % HEAD) // 2, f % 2
    gamma = 1.0 - np.exp(np.linspace(np.log(1.0 / 32.0), np.log(1.0 / 512.0), HEADS))[head]
    scale = ((2.0 * pair + 0.4 * HEAD) / (1.4 * HEAD)) ** (pos / 512.0)
    angle = pos / 10000.0 ** (pair / (HEAD // 2))
    sign = np.where(odd == 1, 1.0, -1.0)
    grow, shrink = scale * gamma ** pos, 1.0 / (scale * gamma ** pos)
    c[:, C_CQ:C_CQ + P] = np.cos(angle) * grow
    c[:, C_SQ:C_SQ + P] = np.sin(angle) * sign * grow
    c[:, C_CK:C_CK + P] = np.cos(angle) * shrink
    c[:, C_SK:C_SK + P] = (np.sin(angle) * sign * shrink)[:, np.arange(P) ^ 1]
    c[:, C_CAUSAL:C_CAUSAL + P] = f >= pos
    c[:, C_IDENT:C_IDENT + P] = f == pos
    c[:, C_BEFORE:C_BEFORE + P] = pos < f
    c[:, C_ONES:C_ONES + P] = 1.0
    c[:, C_IOTA:C_IOTA + E] = np.arange(E)
    c[:, C_BASE:C_BASE + E] = np.arange(E) * REG
    c[:, C_TILE:C_TILE + NT] = np.arange(NT)
    return c.astype(np.float32)


def output_rows():
    s, b, k = np.meshgrid(np.arange(P), np.arange(B), np.arange(K), indexing="ij")
    return np.ascontiguousarray((k * TOK + b * P + s).reshape(P, B * K).astype(np.int32))


def wait(eng, sem, value):
    if not isinstance(value, int) or value > 0:
        eng.wait_ge(sem, value)


def build(nc, x, ctx_in, router_w, router_bias, bank_mag, bank_freq, bank_phase, bank_down, norm_w,
          consts, rows_of, out):
    xg = nc.dram_tensor("routed_rows", (NULL_ROW + P, ROW), F32).ap()
    yg = nc.dram_tensor("expert_outputs", (K * TOK, P), F32).ap()
    x_v = x.rearrange("b s f -> s b f")
    ctx_v = ctx_in.rearrange("b s f -> s b f")
    out_v = out.rearrange("b s f -> s b f")
    yg_v = yg.rearrange("(k b s) f -> s k b f", k=K, b=B)

    with ExitStack() as st:
        def sb(name, cols, dt=F32, parts=P):
            return st.enter_context(nc.sbuf_tensor(name, [parts, cols], dt))

        def sem(name):
            return st.enter_context(nc.semaphore(name))

        cst = sb("cst", C_END)
        rowid = sb("rowid", B * K, I32)
        wmf = sb("wmf", E * 2 * H)
        wdn = sb("wdn", E * 2 * P)
        phase = sb("phase", E * H)
        xa = sb("xa", B * P)
        ca = sb("ca", B * P)
        rw = sb("rw", P, parts=E)
        rwT = sb("rwT", E)
        rbias = sb("rbias", E)
        nw = sb("nw", P)
        causal4 = sb("causal4", 4 * P)
        before_b = sb("before_b", P, BF16)
        ones_b = sb("ones_b", P, BF16)
        halfneg = sb("halfneg", 8)
        pad = sb("pad", ROW)
        st1, mv1, ve1, rstd1 = sb("st1", GRP * 6), sb("mv1", GRP * 2), sb("ve1", GRP), sb("rstd1", GRP)
        st2, mv2, ve2, rstd2 = sb("st2", GRP * 6), sb("mv2", GRP * 2), sb("ve2", GRP), sb("rstd2", GRP)
        xn, q1, q2, k1, k2 = (sb(n, P) for n in ("xn", "q1", "q2", "k1", "k2"))
        turned = sb("turned", 10 * 4 * P)
        qexp, kexp, vexp, qT, kT = ([turned[:, (2 * a + i) * 4 * P:(2 * a + i + 1) * 4 * P] for i in range(2)]
                                    for a in range(5))
        masked = sb("masked", 2 * HEADS * P)
        sm = [masked[:, i * HEADS * P:(i + 1) * HEADS * P] for i in range(2)]
        oT = sb("oT", P)
        xln = sb("xln", GRP * P)
        xlnT = sb("xlnT", GRP * P)
        rowb = sb("rowb", GRP * K * ROW)
        lg = sb("lg", GRP * E)
        mx8, mi8 = sb("mx8", GRP * 8), sb("mi8", GRP * 8, U32)
        ixf = sb("ixf", GRP * K)
        oh = sb("oh", GRP * K * E)
        msel = sb("msel", GRP * E, BF16)
        posb, prod, slf = sb("posb", GRP * E), sb("prod", GRP * K * E), sb("slf", GRP * K)
        sli = sb("sli", GRP * K, I32)
        msum, macc = sb("msum", E), sb("macc", E)
        macc_b = sb("macc_b", E, BF16)
        v12 = sb("v12", B * K)
        wk = sb("wk", K * B)
        wtmp = sb("wtmp", B)
        cnt, cnt_i, nt_i, ntf = sb("cnt", E), sb("cnt_i", E, I32), sb("nt_i", E, I32), sb("ntf", E)
        tend, zero16 = sb("tend", E), sb("zero16", E)
        fill_f, fill_i = sb("fill_f", E), sb("fill_i", E, I32)
        ge = sb("ge", NT * E)
        te, ts_, tb = sb("te", NT), sb("ts_", NT), sb("tb", NT)
        te_i, tb_i = sb("te_i", NT, I32), sb("tb_i", NT, I32)
        xt = [sb(f"xt{i}", TG * ROW) for i in range(2)]
        oid = [sb(f"oid{i}", TG, I32) for i in range(2)]
        xtT = [sb(f"xtT{i}", 2 * P) for i in range(2)]
        th, ex, rr = ([t[:, i * TG * H:(i + 1) * TG * H] for i in range(2)] for t in (turned, masked, ca))
        turn = [sb(f"turn{i}", 2 * H) for i in range(2)]
        hb = [sb(f"hb{i}", 2 * H) for i in range(2)]
        hT = [sb(f"hT{i}", 4 * P) for i in range(2)]
        ob = sb("ob", TG * P)
        o12 = [sb(f"o12_{i}", K * GRP * P) for i in range(2)]
        ym = [sb(f"ym{i}", GRP * P) for i in range(2)]
        ysq = sb("ysq", GRP * P)
        ss, sse, rs3 = (sb(n, 2 * GRP) for n in ("ss", "sse", "rs3"))

        ps = st.enter_context(nc.psum_tensor("ps", [P, 8, 512], F32))
        S4 = [ps[:, g, :] for g in range(4)]
        PQ, PK = ps[:, 4, :], ps[:, 5, :]
        P_OT, P_X2 = ps[:, 6, 0:P], ps[:, 6, :]
        P_O, P_LG, P_POS, P_CNT = ps[:, 7, 0:P], ps[:, 7, P:P + GRP * E], ps[:, 7, 256:256 + GRP * E], ps[:, 7, 384:384 + E]

        identity = cst[:, C_IDENT:C_IDENT + P]

        names = """waited consts_in x_in ctx_in w_in small_in phase_in tables_ready pow_ready zero_ready rw_turned rw_copied
            ln1_stats ln1_mv ln1_var ln1_rstd ln2_stats ln2_mv ln2_var ln2_rstd
            xn_done q_mul q_exp k_mul k_exp q_turned k_turned q_copied k_copied v_exp
            scores_done masked_done av_done ot_copied o_turned x2_done
            xln_done xln_turned xln_copied logits_done
            lg_done max_done maxi_done ixf_done oh_done sel_done pos_done posb_done prod_done slf_done slot_done
            row_copied row_id msum_done macc_done macc_copied rows_scattered v12_done
            cnt_done tab tab_ready wdiff wexp wk_done fills_done pad_ready
            phase_ready
            idx_copied xt_turned xt_copied mf_done abs_done relu_done tanh_done exp_done ln_done sin_done
            theta_sum theta_scaled turns_done theta_done hid_done h_turned h_copied down_done
            y1_done y2_done sq_done rms_var rms_done yn_done out_ready""".split()
        s = {n: sem(n) for n in names}
        xt_in = [sem(f"xt_in{i}") for i in range(2)]
        o_scattered = [sem(f"o_scattered{i}") for i in range(PAIRS)]
        o_copied = sem("o_copied")
        o12_in = [sem(f"o12_in{i}") for i in range(2)]
        out_done = [sem(f"out_done{i}") for i in range(2)]

        def wait_apart(eng, *counts):
            for c, v in counts:
                if not isinstance(v, int) or v > 0:
                    eng.wait_ge(c, v)
                    eng.sem_inc(s["waited"], 1)

        def diag(t, outer, dims):
            return bass.AP(tensor=t.tensor, offset=t.offset, ap=[t.ap[0], [P + outer, 4]] + dims)

        def by_head(t):
            return diag(t, HEAD, [[32, 4], [1, HEAD]])

        def by_group_pairs(t):
            return diag(t, 32, [[2, 16], [1, 2]])

        def head_view(a):
            return a.rearrange("p (g j d) -> p j g d", g=4, j=JH)

        def group_pairs(a):
            return a.rearrange("p (g i two) -> p g i two", g=4, two=2)

        def swap(a):
            return a.rearrange("p (i two) -> p i two", two=2)[:, :, ::-1]

        def pairs(a):
            return a.rearrange("p (i two) -> p i two", two=2)

        def batch(t, n, width=P):
            return t[:, bass.ds(n * width, width)]

        def groups_loop(eng, body):
            body(0)
            body(1)
            with eng.Fori(2, NG - 1) as G:
                body(G)
            for G in range(NG - 1, NG + 2):
                body(G)

        def is_in(G, lo, hi):
            return not isinstance(G, int) or lo <= G < hi

        def tiles_loop(eng, body):
            for T in range(4):
                body(T, T % 2)
            with eng.Fori(2, NTG // 2) as u:
                body(u * 2, 0)
                body(u * 2 + 1, 1)
            body(NTG, 0)
            body(NTG + 1, 1)

        def results_loop(eng, body):
            body(0, 0)
            body(1, 1)
            with eng.Fori(1, NG // 2) as u:
                body(u * 2, 0)
                body(u * 2 + 1, 1)
            body(NG, 0)

        def t_in(T, lo, hi):
            return not isinstance(T, int) or lo <= T < hi

        block = st.enter_context(nc.Block())

        @block.sync
        def _(sp):
            sp.dma_start(cst[:, :], consts).then_inc(s["consts_in"], 16)
            sp.dma_start(rw[:, :], router_w).then_inc(s["small_in"], 16)
            sp.dma_start(rbias[:, :], router_bias.rearrange("(o e) -> o e", o=1).to_broadcast([P, E])).then_inc(s["small_in"], 16)
            sp.dma_start(nw[:, :], norm_w.rearrange("(o f) -> o f", o=1).to_broadcast([P, P])).then_inc(s["small_in"], 16)
            sp.dma_start(rowid[:, :], rows_of).then_inc(s["small_in"], 16)
            with sp.Fori(0, NG) as g:
                sp.dma_start(batch(xa, g, GRP * P).rearrange("p (b f) -> p b f", b=GRP),
                             x_v[:, bass.ds(g * GRP, GRP), :]).then_inc(s["x_in"], 16)
                sp.dma_start(batch(ca, g, GRP * P).rearrange("p (b f) -> p b f", b=GRP),
                             ctx_v[:, bass.ds(g * GRP, GRP), :]).then_inc(s["ctx_in"], 16)
                wait_apart(sp, (s["x_in"], 16 * g + 16), (s["ctx_in"], 16 * g + 16))
            wmf_v = wmf[:, :].rearrange("d (e m h) -> d e m h", e=E, m=2)
            sp.dma_start(wmf_v[:, :, 0, :], bank_mag.rearrange("e d h -> d e h")).then_inc(s["w_in"], 16)
            sp.dma_start(wmf_v[:, :, 1, :], bank_freq.rearrange("e d h -> d e h")).then_inc(s["w_in"], 16)
            sp.dma_start(wdn[:, :].rearrange("p (e c d) -> p e c d", e=E, c=2),
                         bank_down.rearrange("e (c p) d -> p e c d", c=2)).then_inc(s["w_in"], 16)
            sp.dma_start(phase[:, :], bank_phase.rearrange("(o e) h -> o (e h)", o=1).to_broadcast([P, E * H])).then_inc(s["phase_in"], 16)

            sp.wait_ge(s["pad_ready"], 2)
            sp.wait_ge(s["tab_ready"], 1)
            sp.dma_start(xg[NULL_ROW:NULL_ROW + P, :], pad[:, :]).then_inc(s["fills_done"], 16)
            with sp.Fori(0, E) as e:
                row = sp.value_load(fill_i[0:1, bass.ds(e, 1)], min_val=0, max_val=NULL_ROW - P)
                sp.dma_start(xg[bass.ds(row, P), :], pad[:, :]).then_inc(s["fills_done"], 16)
            sp.wait_ge(s["fills_done"], 16 * (E + 1))
            sp.wait_ge(s["rows_scattered"], 16 * GRP * K * NG)

            def tiles(T, par):
                if not t_in(T, 0, NTG):
                    return
                wait_apart(sp, (s["idx_copied"], T - 1), (s["xt_turned"], PAIRS * (T - 1)))
                for i in range(TG):
                    base = sp.value_load(tb_i[0:1, bass.ds(T * TG + i, 1)], min_val=0, max_val=NULL_ROW)
                    sp.dma_start(xt[par][:, i * ROW:(i + 1) * ROW], xg[bass.ds(base, P), :]).then_inc(xt_in[par], 16)
            tiles_loop(sp, tiles)

            for p in range(PAIRS):
                sp.wait_ge(o_scattered[p], 32 * NTG)

            def outputs_of(g, par):
                if not t_in(g, 0, NG):
                    return
                wait_apart(sp, (s["y2_done"], GRP * (g - 1)))
                for k in range(K):
                    sp.dma_start(o12[par][:, k * GRP * P:(k + 1) * GRP * P].rearrange("p (b f) -> p b f", b=GRP),
                                 yg_v[:, k, bass.ds(g * GRP, GRP), :]).then_inc(o12_in[par], 16)
            results_loop(sp, outputs_of)

        @block.tensor
        def _(pe):
            pe.wait_ge(s["consts_in"], 16)
            pe.wait_ge(s["small_in"], 64)
            pe.transpose(P_LG[:, 0:E], rw[:, :], identity[0:E, 0:E]).then_inc(s["rw_turned"], 1)

            def turn_qk(m, par):
                pe.wait_ge(s["q_exp"], m + 1)
                wait(pe, s["q_copied"], m)
                for j in range(4):
                    mm = pe.transpose(PQ[:, j * P:(j + 1) * P], qexp[par][:, j * P:(j + 1) * P], identity)
                mm.then_inc(s["q_turned"], 1)
                pe.wait_ge(s["k_exp"], m + 1)
                wait(pe, s["k_copied"], m)
                for g in range(4):
                    mm = pe.transpose(PK[:, g * P:(g + 1) * P], kexp[par][:, g * P:(g + 1) * P], identity)
                mm.then_inc(s["k_turned"], 1)

            def scores(n, par):
                pe.wait_ge(s["q_copied"], n + 1)
                pe.wait_ge(s["k_copied"], n + 1)
                for g in range(4):
                    wait(pe, s["masked_done"], 4 * n + g - 3)
                    pe.matmul(S4[g], kT[par][:, g * P:(g + 1) * P], qT[par][:, :],
                              start=True, stop=True).then_inc(s["scores_done"], 1)

            def values(n, par, turned_groups):
                pe.wait_ge(s["masked_done"], 4 * n + 4)
                pe.wait_ge(s["v_exp"], n + 1)
                wait(pe, s["ot_copied"], n)
                wait(pe, s["xln_copied"], turned_groups)
                for j in range(JH):
                    for g in range(4):
                        mm = pe.matmul(P_OT[32 * g:32 * g + 32, :], vexp[par][:, j * P + 32 * g:j * P + 32 * g + 32],
                                       sm[par][:, (4 * g + j) * P:(4 * g + j + 1) * P],
                                       start=(j == 0), stop=(j == JH - 1))
                mm.then_inc(s["av_done"], 1)

            def turn_o(n, lg_groups, pos_groups):
                pe.wait_ge(s["ot_copied"], n + 1)
                wait(pe, s["x2_done"], n)
                wait(pe, s["lg_done"], lg_groups)
                wait(pe, s["posb_done"], pos_groups)
                pe.transpose(P_O, oT[:, :], identity).then_inc(s["o_turned"], 1)

            def turn_xln(R):
                pe.wait_ge(s["xln_done"], GRP * R + GRP)
                wait(pe, s["ot_copied"], GRP * R + 6 if not isinstance(R, int) else min(GRP * R + 6, B))
                for b in range(GRP):
                    mm = pe.transpose(P_X2[:, b * P:(b + 1) * P], xln[:, b * P:(b + 1) * P], identity)
                mm.then_inc(s["xln_turned"], 1)

            def logits(R):
                pe.wait_ge(s["xln_copied"], R + 1)
                pe.wait_ge(s["x2_done"], GRP * R + 6 if not isinstance(R, int) else min(GRP * R + 6, B))
                for b in range(GRP):
                    mm = pe.matmul(P_LG[:, b * E:(b + 1) * E], xlnT[:, b * P:(b + 1) * P], rwT[:, :], start=True, stop=True)
                mm.then_inc(s["logits_done"], 1)

            def positions(R):
                pe.wait_ge(s["sel_done"], R + 1)
                pe.wait_ge(s["macc_copied"], R + 1)
                pe.wait_ge(s["x2_done"], GRP * R + 8 if not isinstance(R, int) else min(GRP * R + 8, B))
                pe.matmul(P_POS, before_b[:, :], msel[:, :], start=True, stop=False)
                for b in range(GRP - 1):
                    pe.matmul(P_POS[:, (b + 1) * E:].rearrange("p (b e) -> p b e", e=E), ones_b[:, :],
                              msel[:, b * E:(b + 1) * E].unsqueeze(1).to_broadcast([P, GRP - 1 - b, E]), start=False, stop=False)
                pe.matmul(P_POS.rearrange("p (b e) -> p b e", e=E), ones_b[:, :],
                          macc_b[:, :].unsqueeze(1).to_broadcast([P, GRP, E]), start=False, stop=True).then_inc(s["pos_done"], 1)

            pe.wait_ge(s["rw_copied"], 1)
            turn_qk(0, 0)

            def body(G):
                for i in range(GRP):
                    n = GRP * G + i
                    if is_in(G, 0, NG):
                        scores(n, i % 2)
                    if i == 3 and is_in(G, 1, NG + 1):
                        turn_xln(G - 1)
                    if is_in(G, 0, NG) and not (isinstance(G, int) and n + 1 >= B):
                        turn_qk(n + 1, (i + 1) % 2)
                    if not isinstance(G, int) or 0 <= n - 2 < B:
                        turn_o(n - 2, G - 1, G - 1 if i >= 2 else G - 2)
                    if not isinstance(G, int) or 0 <= n - 1 < B:
                        values(n - 1, (i + 1) % 2, G if i == 3 else G - 1)
                    if i == 3 and is_in(G, 1, NG + 1):
                        logits(G - 1)
                    if i == 1 and is_in(G, 2, NG + 2):
                        positions(G - 2)
            groups_loop(pe, body)

            pe.wait_ge(s["macc_copied"], NG + 1)
            pe.matmul(P_CNT, ones_b[:, :], macc_b[:, :], start=True, stop=True).then_inc(s["cnt_done"], 1)

            pe.wait_ge(s["w_in"], 48)
            pe.wait_ge(s["tab_ready"], 1)

            def tiles(T, par):
                def expert(t):
                    return pe.value_load(te_i[0:1, bass.ds(t, 1)], min_val=0, max_val=E - 1)
                for p in range(PAIRS):
                    q = p % 2
                    if t_in(T, 0, NTG):
                        if p == 0:
                            pe.wait_ge(xt_in[par], 64 * (T - par) + 128)
                        wait(pe, s["xt_copied"], PAIRS * T + p)
                        for i in range(2):
                            t = 2 * p + i
                            mm = pe.transpose(ps[:, 4, i * P:(i + 1) * P], xt[par][:, t * ROW:t * ROW + P], identity)
                        mm.then_inc(s["xt_turned"], 1)
                    if t_in(T, 2, NTG + 2):
                        pe.wait_ge(s["hid_done"], PAIRS * (T - 2) + p + 1)
                        wait(pe, s["h_copied"], PAIRS * (T - 2) + p)
                        for c in range(4):
                            mm = pe.transpose(ps[:, 5, c * P:(c + 1) * P], hb[q][:, c * P:(c + 1) * P], identity)
                        mm.then_inc(s["h_turned"], 1)
                    if t_in(T, 0, NTG):
                        wait(pe, s["tanh_done"], PAIRS * T + p - 1)
                        wait(pe, s["abs_done"], PAIRS * T + p - 1)
                        wait(pe, s["relu_done"], 2 * (PAIRS * T + p - 1))
                        pe.wait_ge(s["xt_copied"], PAIRS * T + p + 1)
                        for i in range(2):
                            e = expert(T * TG + 2 * p + i)
                            for m in range(2):
                                mm = pe.matmul(ps[:, 2 * q + m, i * H:(i + 1) * H], xtT[q][:, i * P:(i + 1) * P],
                                               wmf[:, bass.ds(e * (2 * H) + m * H, H)], start=True, stop=True)
                        mm.then_inc(s["mf_done"], 1)
                    if t_in(T, 2, NTG + 2):
                        pe.wait_ge(s["h_copied"], PAIRS * (T - 2) + p + 1)
                        wait(pe, o_copied, PAIRS * (T - 2) + p)
                        for i in range(2):
                            e = expert((T - 2) * TG + 2 * p + i)
                            for c in range(2):
                                mm = pe.matmul(ps[:, 6, i * P:(i + 1) * P], hT[q][:, (2 * i + c) * P:(2 * i + c + 1) * P],
                                               wdn[:, bass.ds(e * (2 * P) + c * P, P)], start=(c == 0), stop=(c == 1))
                        mm.then_inc(s["down_done"], 1)
            tiles_loop(pe, tiles)

        @block.scalar
        def _(act):
            act.wait_ge(s["rw_turned"], 1)
            act.copy(rwT[:, :], P_LG[:, 0:E]).then_inc(s["rw_copied"], 1)

            def take_qk(m, par):
                act.wait_ge(s["q_turned"], m + 1)
                wait(act, s["scores_done"], 4 * (m - 1))
                act.copy(qT[par][:, :], PQ).then_inc(s["q_copied"], 1)
                act.wait_ge(s["k_turned"], m + 1)
                act.copy(kT[par][:, :], PK).then_inc(s["k_copied"], 1)

            def expand_v(m, g, par):
                act.wait_ge(s["ctx_in"], 16 * g + 16)
                wait(act, s["av_done"], m - 1)
                act.copy(by_head(vexp[par]), head_view(batch(ca, m))).then_inc(s["v_exp"], 1)

            act.wait_ge(s["zero_ready"], ZEROED)
            take_qk(0, 0)
            expand_v(0, 0, 0)

            def body(G):
                for i in range(GRP):
                    n = GRP * G + i
                    more = is_in(G, 0, NG) and not (isinstance(G, int) and n + 1 >= B)
                    if more:
                        take_qk(n + 1, (i + 1) % 2)
                    if i == 3 and is_in(G, 1, NG + 1):
                        act.wait_ge(s["xln_turned"], G)
                        wait(act, s["logits_done"], G - 1)
                        act.copy(xlnT[:, :], P_X2).then_inc(s["xln_copied"], 1)
                    if not isinstance(G, int) or 0 <= n - 1 < B:
                        act.wait_ge(s["av_done"], n)
                        wait(act, s["o_turned"], n - 1)
                        act.copy(oT[:, :], P_OT).then_inc(s["ot_copied"], 1)
                    if more:
                        expand_v(n + 1, G + (i + 1) // GRP, (i + 1) % 2)
            groups_loop(act, body)

            act.wait_ge(s["wdiff"], 1)
            act.activation(wtmp[:, :], wtmp[:, :], ACT.Exp).then_inc(s["wexp"], 1)

            def tiles(T, par):
                for p in range(PAIRS):
                    q = p % 2
                    if t_in(T, 0, NTG):
                        act.wait_ge(s["xt_turned"], PAIRS * T + p + 1)
                        wait(act, s["mf_done"], PAIRS * T + p - 1)
                        act.copy(xtT[q][:, :], ps[:, 4, 0:2 * P]).then_inc(s["xt_copied"], 1)
                    if t_in(T, 2, NTG + 2):
                        act.wait_ge(s["h_turned"], PAIRS * (T - 2) + p + 1)
                        wait(act, s["down_done"], PAIRS * (T - 2) + p - 1)
                        act.copy(hT[q][:, :], ps[:, 5, :]).then_inc(s["h_copied"], 1)
                    if t_in(T, 0, NTG):
                        act.wait_ge(s["mf_done"], PAIRS * T + p + 1)
                        wait(act, s["hid_done"], PAIRS * (T - 2) + p + 1)
                        act.activation(th[par][:, p * 2 * H:(p + 1) * 2 * H], ps[:, 2 * q, :], ACT.Tanh).then_inc(s["tanh_done"], 1)
                        act.wait_ge(s["abs_done"], PAIRS * T + p + 1)
                        act.activation(ex[par][:, p * 2 * H:(p + 1) * 2 * H], ex[par][:, p * 2 * H:(p + 1) * 2 * H],
                                       ACT.Exp, scale=-1.0).then_inc(s["exp_done"], 1)
                    if t_in(T, 2, NTG + 2):
                        act.wait_ge(s["down_done"], PAIRS * (T - 2) + p + 1)
                        wait(act, o_scattered[p], 32 * (T - 2))
                        act.copy(ob[:, 2 * p * P:(2 * p + 2) * P], ps[:, 6, 0:2 * P]).then_inc(o_copied, 1)
                if t_in(T, 0, NTG):
                    act.wait_ge(s["exp_done"], PAIRS * T + PAIRS)
                    act.activation(ex[par][:, :], ex[par][:, :], ACT.Ln, bias=1.0).then_inc(s["ln_done"], 1)
                if t_in(T, 1, NTG + 1):
                    act.wait_ge(s["theta_done"], PAIRS * T)
                    act.activation(rr[1 - par][:, :], rr[1 - par][:, :], ACT.Sin).then_inc(s["sin_done"], 1)
            tiles_loop(act, tiles)

            def results(g, par):
                if t_in(g, 0, NG):
                    wait(act, s["rms_var"], g - 1)
                    wait(act, s["sq_done"], GRP * g)
                    for b in range(GRP):
                        act.wait_ge(s["y2_done"], GRP * g + b + 1)
                        act.activation(ysq[:, b * P:(b + 1) * P], ym[par][:, b * P:(b + 1) * P], ACT.Square,
                                       accum_out=ss[:, par * GRP + b:par * GRP + b + 1]).then_inc(s["sq_done"], 1)
                if t_in(g, 1, NG + 1):
                    act.wait_ge(s["out_ready"], g)
                    act.dma_start(out_v[:, bass.ds((g - 1) * GRP, GRP), :],
                                  ym[1 - par][:, :].rearrange("p (b f) -> p b f", b=GRP)).then_inc(out_done[1 - par], 16)
            results_loop(act, results)
            for par in range(2):
                act.wait_ge(out_done[par], 16 * NG // 2)

        @block.vector
        def _(dve):
            for t in qexp:
                dve.memset(t[:, :], 0.0).then_inc(s["zero_ready"], 1)
            dve.memset(rowb[:, :], 0.0).then_inc(s["zero_ready"], 1)
            dve.memset(macc[:, :], 0.0).then_inc(s["macc_done"], 1)
            dve.memset(macc_b[:, :], 0.0).then_inc(s["macc_copied"], 1)
            dve.memset(zero16[:, :], 0.0).then_inc(s["zero_ready"], 1)
            dve.memset(pad[:, 0:P], 0.0).then_inc(s["pad_ready"], 1)
            dve.memset(pad[:, P:ROW].bitcast(I32), DROP).then_inc(s["pad_ready"], 1)
            dve.wait_ge(s["consts_in"], 16)
            dve.tensor_copy(causal4[:, :].rearrange("p (j s) -> p j s", j=4),
                            cst[:, C_CAUSAL:C_CAUSAL + P].unsqueeze(1).to_broadcast([P, 4, P])).then_inc(s["tables_ready"], 1)
            dve.tensor_copy(before_b[:, :], cst[:, C_BEFORE:C_BEFORE + P]).then_inc(s["tables_ready"], 1)
            dve.tensor_copy(ones_b[:, :], cst[:, C_ONES:C_ONES + P]).then_inc(s["tables_ready"], 1)

            def stats(xs, stt_, mv, ve, names, count):
                for b in range(GRP):
                    dve.bn_stats(stt_[:, 6 * b:6 * b + 6], xs(b)).then_inc(s[names[0]], 1)
                for b in range(GRP):
                    wait_apart(dve, (s[names[0]], GRP * count + b + 1))
                    dve.bn_aggr(mv[:, 2 * b:2 * b + 2], stt_[:, 6 * b:6 * b + 6]).then_inc(s[names[1]], 1)
                dve.wait_ge(s[names[1]], GRP * count + GRP)
                dve.tensor_scalar(ve[:, :], mv[:, 1:2 * GRP:2], LN_EPS, None, ALU.add).then_inc(s[names[2]], 1)

            def stats1(g):
                dve.wait_ge(s["x_in"], 16 * g + 16)
                stats(lambda b: batch(xa, GRP * g + b), st1, mv1, ve1, ["ln1_stats", "ln1_mv", "ln1_var"], g)

            def rotate_q(m, g, i):
                if i == 0:
                    dve.wait_ge(s["ln1_rstd"], g + 1)
                wait(dve, s["q_mul"], 2 * m)
                dve.tensor_scalar(xn[:, :], batch(xa, m), mv1[:, 2 * i:2 * i + 1], rstd1[:, i:i + 1],
                                  ALU.subtract, ALU.mult).then_inc(s["xn_done"], 1)
                wait(dve, s["q_exp"], m)
                dve.wait_ge(s["xn_done"], m + 1)
                dve.tensor_tensor(q1[:, :], xn[:, :], cst[:, C_CQ:C_CQ + P], ALU.mult).then_inc(s["q_mul"], 1)
                dve.tensor_tensor(pairs(q2[:, :]), swap(xn[:, :]), pairs(cst[:, C_SQ:C_SQ + P]), ALU.mult).then_inc(s["q_mul"], 1)
                dve.wait_ge(s["q_mul"], 2 * m + 2)
                wait(dve, s["q_turned"], m - 1)
                dve.tensor_tensor(by_head(qexp[i % 2]), head_view(q1[:, :]), head_view(q2[:, :]), ALU.add).then_inc(s["q_exp"], 1)

            stats1(0)
            dve.wait_ge(s["zero_ready"], ZEROED)
            for i in range(2):
                rotate_q(i, 0, i)

            def mask(n, par):
                wait(dve, s["av_done"], n - 1)
                for g in range(4):
                    dve.wait_ge(s["scores_done"], 4 * n + g + 1)
                    dve.tensor_tensor(sm[par][:, g * 4 * P:(g + 1) * 4 * P], S4[g], causal4[:, :],
                                      ALU.mult).then_inc(s["masked_done"], 1)

            def add_attention(n):
                dve.wait_ge(s["o_turned"], n + 1)
                dve.tensor_tensor(batch(xa, n), batch(xa, n), P_O, ALU.add).then_inc(s["x2_done"], 1)

            def stats2(R):
                dve.wait_ge(s["x2_done"], GRP * R + GRP)
                stats(lambda b: batch(xa, GRP * R + b), st2, mv2, ve2, ["ln2_stats", "ln2_mv", "ln2_var"], R)

            def normalise(R):
                dve.wait_ge(s["ln2_rstd"], R + 1)
                wait(dve, s["row_copied"], R)
                for b in range(GRP):
                    dve.tensor_scalar(xln[:, b * P:(b + 1) * P], batch(xa, GRP * R + b), mv2[:, 2 * b:2 * b + 1],
                                      rstd2[:, b:b + 1], ALU.subtract, ALU.mult).then_inc(s["xln_done"], 1)

            lg3 = lg[:, :].rearrange("p (b e) -> p b e", b=GRP)
            oh4 = oh[:, :].rearrange("p (b k e) -> p b k e", b=GRP, k=K)
            msel3 = msel[:, :].rearrange("p (b e) -> p b e", b=GRP)
            posb3 = posb[:, :].rearrange("p (b e) -> p b e", b=GRP)
            mx3 = mx8[:, :].rearrange("p (b r) -> p b r", b=GRP)
            mi3 = mi8[:, :].rearrange("p (b r) -> p b r", b=GRP)
            iota = cst[:, C_IOTA:C_IOTA + E].unsqueeze(1).unsqueeze(1)
            base = cst[:, C_BASE:C_BASE + E].unsqueeze(1)

            def take_logits(R):
                dve.wait_ge(s["logits_done"], R + 1)
                dve.tensor_tensor(lg3, P_LG.rearrange("p (b e) -> p b e", b=GRP),
                                  rbias[:, :].unsqueeze(1).to_broadcast([P, GRP, E]), ALU.add).then_inc(s["lg_done"], 1)

            def choose(R):
                wait_apart(dve, (s["lg_done"], R + 1))
                for b in range(GRP):
                    dve.max(mx3[:, b, :], lg3[:, b, :]).then_inc(s["max_done"], 1)
                for b in range(GRP):
                    wait_apart(dve, (s["max_done"], GRP * R + b + 1))
                    dve.max_index(mi3[:, b, :], mx3[:, b, :], lg3[:, b, :]).then_inc(s["maxi_done"], 1)
                dve.wait_ge(s["maxi_done"], GRP * R + GRP)
                dve.tensor_copy(ixf[:, :].rearrange("p (b k) -> p b k", k=K), mi3[:, :, 0:K]).then_inc(s["ixf_done"], 1)
                dve.tensor_copy(batch(v12, R, GRP * K).rearrange("p (b k) -> p b k", k=K), mx3[:, :, 0:K]).then_inc(s["v12_done"], 1)
                dve.wait_ge(s["ixf_done"], R + 1)
                dve.tensor_tensor(oh4, iota.to_broadcast([P, GRP, K, E]),
                                  ixf[:, :].rearrange("p (b k) -> p b k", k=K).unsqueeze(3).to_broadcast([P, GRP, K, E]),
                                  ALU.is_equal).then_inc(s["oh_done"], 1)
                dve.wait_ge(s["oh_done"], R + 1)
                dve.tensor_tensor(msel3, oh4[:, :, 0, :], oh4[:, :, 1, :], ALU.add).then_inc(s["sel_done"], 1)

            def take_positions(R):
                dve.wait_ge(s["pos_done"], R + 1)
                dve.tensor_tensor(posb3, P_POS.rearrange("p (b e) -> p b e", b=GRP), base.to_broadcast([P, GRP, E]),
                                  ALU.add).then_inc(s["posb_done"], 1)

            def place(R):
                dve.tensor_reduce(msum[:, :], msel3.rearrange("p b e -> p e b"), AX.X, ALU.add).then_inc(s["msum_done"], 1)
                dve.wait_ge(s["posb_done"], R + 1)
                dve.tensor_tensor(prod[:, :].rearrange("p (b k e) -> p b k e", b=GRP, k=K), oh4,
                                  posb3.unsqueeze(2).to_broadcast([P, GRP, K, E]), ALU.mult).then_inc(s["prod_done"], 1)
                dve.wait_ge(s["msum_done"], R + 1)
                dve.wait_ge(s["macc_done"], R + 1)
                dve.tensor_tensor(macc[:, :], macc[:, :], msum[:, :], ALU.add).then_inc(s["macc_done"], 1)
                dve.wait_ge(s["prod_done"], R + 1)
                dve.tensor_reduce(slf[:, :], prod[:, :].rearrange("p (c e) -> p c e", e=E), AX.X, ALU.add).then_inc(s["slf_done"], 1)
                dve.wait_ge(s["macc_done"], R + 2)
                dve.tensor_copy(macc_b[:, :], macc[:, :]).then_inc(s["macc_copied"], 1)
                dve.wait_ge(s["slf_done"], R + 1)
                wait(dve, s["rows_scattered"], 16 * GRP * K * R)
                dve.tensor_copy(sli[:, :], slf[:, :]).then_inc(s["slot_done"], 1)
                rows = rowb[:, :].rearrange("p (b k w) -> p b k w", b=GRP, k=K)
                dve.wait_ge(s["xln_done"], GRP * R + GRP)
                dve.tensor_copy(rows[:, :, :, 0:P], xln[:, :].rearrange("p (b f) -> p b f", b=GRP).unsqueeze(2)
                                .to_broadcast([P, GRP, K, P])).then_inc(s["row_copied"], 1)
                dve.tensor_copy(rowb[:, :].rearrange("p (c w) -> p c w", w=ROW)[:, :, P].bitcast(I32),
                                batch(rowid, R, GRP * K)).then_inc(s["row_id"], 1)

            def body(G):
                for i in range(GRP):
                    n = GRP * G + i
                    if i == 0 and is_in(G, 2, NG + 2):
                        take_logits(G - 2)
                    if i == 2 and is_in(G, 2, NG + 2):
                        take_positions(G - 2)
                    if is_in(G, 0, NG):
                        mask(n, i % 2)
                        if not (isinstance(G, int) and n + 2 >= B):
                            rotate_q(n + 2, G + (i + 2) // GRP, (i + 2) % GRP)
                    if not isinstance(G, int) or 0 <= n - 2 < B:
                        add_attention(n - 2)
                    if i == 0 and is_in(G, 2, NG + 2):
                        choose(G - 2)
                    if i == 1:
                        if is_in(G, 0, NG - 1):
                            stats1(G + 1)
                        if is_in(G, 1, NG + 1):
                            stats2(G - 1)
                    if i == 2 and is_in(G, 2, NG + 2):
                        place(G - 2)
                    if i == 2 and is_in(G, 1, NG + 1):
                        normalise(G - 1)
            groups_loop(dve, body)

            done = [0]

            def step(ins):
                done[0] += 1
                ins.then_inc(s["tab"], 1)
                dve.wait_ge(s["tab"], done[0])
            dve.wait_ge(s["cnt_done"], 1)
            step(dve.tensor_copy(cnt[:, :], P_CNT))
            step(dve.tensor_tensor(fill_f[:, :], cnt[:, :], cst[:, C_BASE:C_BASE + E], ALU.add))
            step(dve.tensor_copy(fill_i[:, :], fill_f[:, :]))
            step(dve.tensor_scalar(cnt[:, :], cnt[:, :], float(P - 1), None, ALU.add))
            step(dve.tensor_copy(cnt_i[:, :], cnt[:, :]))
            step(dve.tensor_scalar(nt_i[:, :], cnt_i[:, :], 7, None, ALU.logical_shift_right))
            step(dve.tensor_copy(ntf[:, :], nt_i[:, :]))
            step(dve.tensor_tensor_scan(tend[:, :], ntf[:, :], zero16[:, :], 0.0, ALU.add, ALU.add))
            g1 = ge[0:1, :].rearrange("o (t e) -> o t e", e=E)
            step(dve.tensor_tensor(g1, cst[0:1, C_TILE:C_TILE + NT].unsqueeze(2).to_broadcast([1, NT, E]),
                                   tend[0:1, :].unsqueeze(1).to_broadcast([1, NT, E]), ALU.is_ge))
            step(dve.tensor_reduce(te[0:1, :], g1, AX.X, ALU.add))
            step(dve.tensor_tensor(g1, g1, ntf[0:1, :].unsqueeze(1).to_broadcast([1, NT, E]), ALU.mult))
            step(dve.tensor_reduce(ts_[0:1, :], g1, AX.X, ALU.add))
            step(dve.tensor_tensor(ts_[0:1, :], cst[0:1, C_TILE:C_TILE + NT], ts_[0:1, :], ALU.subtract))
            step(dve.tensor_scalar(ts_[0:1, :], ts_[0:1, :], float(P), None, ALU.mult))
            step(dve.scalar_tensor_tensor(out=tb[0:1, :], in0=te[0:1, :], scalar=float(REG), in1=ts_[0:1, :],
                                          op0=ALU.mult, op1=ALU.add))
            step(dve.tensor_scalar(tb[0:1, :], tb[0:1, :], float(NULL_ROW), None, ALU.min))
            step(dve.tensor_copy(tb_i[0:1, :], tb[0:1, :]))
            step(dve.tensor_scalar(te[0:1, :], te[0:1, :], float(E - 1), None, ALU.min))
            dve.tensor_copy(te_i[0:1, :], te[0:1, :]).then_inc(s["tab_ready"], 1)

            v3 = v12[:, :].rearrange("p (b k) -> p b k", k=K)
            dve.wait_ge(s["v12_done"], NG)
            dve.tensor_tensor(wtmp[:, :], v3[:, :, 1], v3[:, :, 0], ALU.subtract).then_inc(s["wdiff"], 1)
            dve.wait_ge(s["wexp"], 1)
            step(dve.tensor_scalar(wk[:, B:2 * B], wtmp[:, :], 1.0, None, ALU.add))
            step(dve.reciprocal(wk[:, 0:B], wk[:, B:2 * B]))
            dve.tensor_tensor(wk[:, B:2 * B], wtmp[:, :], wk[:, 0:B], ALU.mult).then_inc(s["wk_done"], 1)

            dve.wait_ge(s["phase_in"], 16)
            dve.tensor_scalar(phase[:, :], phase[:, :], float(0.1 + np.pi / 2), None, ALU.add).then_inc(s["phase_ready"], 1)
            dve.wait_ge(s["phase_ready"], 1)
            dve.wait_ge(s["tab_ready"], 1)

            def tiles(T, par):
                for p in range(PAIRS):
                    q = p % 2
                    cols = slice(p * 2 * H, (p + 1) * 2 * H)
                    if t_in(T, 2, NTG + 2):
                        dve.wait_ge(s["sin_done"], T - 1)
                        wait(dve, s["h_turned"], PAIRS * (T - 2) + p - 1)
                        dve.tensor_tensor(hb[q][:, :], th[par][:, cols], rr[par][:, cols], ALU.mult).then_inc(s["hid_done"], 1)
                    if t_in(T, 0, NTG):
                        dve.wait_ge(s["mf_done"], PAIRS * T + p + 1)
                        freq = ps[:, 2 * q + 1, :]
                        dve.tensor_scalar(ex[par][:, cols].bitcast(I32), freq.bitcast(I32),
                                          0x7FFFFFFF, None, ALU.bitwise_and).then_inc(s["abs_done"], 1)
                        for i in range(2):
                            e = dve.value_load(te_i[0:1, bass.ds(T * TG + 2 * p + i, 1)], min_val=0, max_val=E - 1)
                            dve.wait_ge(s["hid_done"], PAIRS * (T - 2) + p + 1) if t_in(T, 2, NTG) else None
                            dve.scalar_tensor_tensor(out=rr[par][:, (2 * p + i) * H:(2 * p + i + 1) * H],
                                                     in0=freq[:, i * H:(i + 1) * H], scalar=0.0,
                                                     in1=phase[:, bass.ds(e * H, H)], op0=ALU.max,
                                                     op1=ALU.add).then_inc(s["relu_done"], 1)
                    if t_in(T, 1, NTG + 1):
                        dve.wait_ge(s["ln_done"], T)
                        dve.wait_ge(s["relu_done"], 2 * (PAIRS * (T - 1) + p) + 2)
                        dve.tensor_tensor(rr[1 - par][:, cols], rr[1 - par][:, cols], ex[1 - par][:, cols],
                                          ALU.add).then_inc(s["theta_sum"], 1)
                        if p:
                            finish(T - 1, 1 - par, p - 1)
                if t_in(T, 1, NTG + 1):
                    finish(T - 1, 1 - par, PAIRS - 1)

            def finish(T, par, p):
                cols = slice(p * 2 * H, (p + 1) * 2 * H)
                dve.wait_ge(s["turns_done"], PAIRS * T + p + 1)
                dve.tensor_tensor(rr[par][:, cols], rr[par][:, cols], turn[p % 2][:, :], ALU.add).then_inc(s["theta_done"], 1)
            tiles_loop(dve, tiles)

            dve.wait_ge(s["wk_done"], 1)

            def results(g, par):
                if t_in(g, 0, NG):
                    dve.wait_ge(o12_in[par], 16 * (g - par) + 32)
                    wait(dve, out_done[par], 8 * (g - par))
                    for b in range(GRP):
                        dve.tensor_scalar(ym[par][:, b * P:(b + 1) * P], o12[par][:, b * P:(b + 1) * P],
                                          wk[:, bass.ds(g * GRP + b, 1)], None, ALU.mult).then_inc(s["y1_done"], 1)
                    for b in range(GRP):
                        dve.wait_ge(s["y1_done"], GRP * g + b + 1)
                        dve.scalar_tensor_tensor(out=ym[par][:, b * P:(b + 1) * P],
                                                 in0=o12[par][:, (GRP + b) * P:(GRP + b + 1) * P],
                                                 scalar=wk[:, bass.ds(B + g * GRP + b, 1)], in1=ym[par][:, b * P:(b + 1) * P],
                                                 op0=ALU.mult, op1=ALU.add).then_inc(s["y2_done"], 1)
                    dve.wait_ge(s["sq_done"], GRP * g + GRP)
                    dve.tensor_scalar(sse[:, par * GRP:(par + 1) * GRP], ss[:, par * GRP:(par + 1) * GRP],
                                      1.0 / P, RMS_EPS, ALU.mult, ALU.add).then_inc(s["rms_var"], 1)
                if t_in(g, 1, NG + 1):
                    h = 1 - par
                    dve.wait_ge(s["rms_done"], g)
                    for b in range(GRP):
                        dve.scalar_tensor_tensor(out=ym[h][:, b * P:(b + 1) * P], in0=ym[h][:, b * P:(b + 1) * P],
                                                 scalar=rs3[:, h * GRP + b:h * GRP + b + 1], in1=nw[:, :],
                                                 op0=ALU.mult, op1=ALU.mult).then_inc(s["yn_done"], 1)
                    dve.wait_ge(s["yn_done"], GRP * g)
                    dve.tensor_tensor(ym[h][:, :], ym[h][:, :], batch(xa, g - 1, GRP * P), ALU.add).then_inc(s["out_ready"], 1)
            results_loop(dve, results)

        @block.gpsimd
        def _(pool):
            for t in kexp + vexp:
                pool.memset(t, 0.0).then_inc(s["zero_ready"], 1)
            pool.memset(halfneg[:, :], -0.5).then_inc(s["pow_ready"], 1)
            pool.wait_ge(s["pow_ready"], 1)
            pool.wait_ge(s["consts_in"], 16)

            def root(var_sem, rstd_sem, out_, in_, count):
                pool.wait_ge(var_sem, count + 1)
                pool.tensor_tensor(out_, in_, halfneg[:, 0:GRP], ALU.pow).then_inc(rstd_sem, 1)

            def rotate_k(m, g, par):
                pool.wait_ge(s["ctx_in"], 16 * g + 16)
                wait(pool, s["k_exp"], m)
                pool.tensor_tensor(k1[:, :], batch(ca, m), cst[:, C_CK:C_CK + P], ALU.mult).then_inc(s["k_mul"], 1)
                pool.tensor_tensor(k2[:, :], batch(ca, m), cst[:, C_SK:C_SK + P], ALU.mult).then_inc(s["k_mul"], 1)
                pool.wait_ge(s["k_mul"], 2 * m + 2)
                wait(pool, s["k_turned"], m - 1)
                pool.tensor_tensor(by_group_pairs(kexp[par]), group_pairs(k1[:, :]), group_pairs(k2[:, :])[:, :, :, ::-1],
                                   ALU.add).then_inc(s["k_exp"], 1)

            def scatter(R, first, last):
                if first == 0:
                    wait_apart(pool, (s["slot_done"], R + 1), (s["row_copied"], R + 1), (s["row_id"], R + 1))
                for c in range(first, last):
                    pool.indirect_dma_start(xg, bass.IndirectOffsetOnAxis(ap=sli[:, c:c + 1], axis=0),
                                            rowb[:, c * ROW:(c + 1) * ROW], None,
                                            bounds_check=NULL_ROW - 1, oob_is_err=False).then_inc(s["rows_scattered"], 16)

            pool.wait_ge(s["zero_ready"], ZEROED)
            root(s["ln1_var"], s["ln1_rstd"], rstd1[:, :], ve1[:, :], 0)
            for i in range(2):
                rotate_k(i, 0, i)

            def body(G):
                for i in range(GRP):
                    n = GRP * G + i
                    if is_in(G, 0, NG) and not (isinstance(G, int) and n + 2 >= B):
                        rotate_k(n + 2, G + (i + 2) // GRP, i % 2)
                    if i == 1:
                        if is_in(G, 0, NG - 1):
                            root(s["ln1_var"], s["ln1_rstd"], rstd1[:, :], ve1[:, :], G + 1)
                        if is_in(G, 1, NG + 1):
                            root(s["ln2_var"], s["ln2_rstd"], rstd2[:, :], ve2[:, :], G - 1)
                    if is_in(G, 2, NG + 2):
                        if i == 2:
                            scatter(G - 2, 0, 4)
                        if i == 3:
                            scatter(G - 2, 4, 8)
            groups_loop(pool, body)

            def tiles(T, par):
                for p in range(PAIRS):
                    if t_in(T, 1, NTG + 1):
                        m = PAIRS * (T - 1) + p
                        cols = slice(p * 2 * H, (p + 1) * 2 * H)
                        wait_apart(pool, (s["theta_sum"], m + 1), (s["theta_done"], m - 1))
                        pool.tensor_scalar(turn[p % 2][:, :], rr[1 - par][:, cols], float(1 / TWO_PI), float(MAGIC),
                                           ALU.mult, ALU.add).then_inc(s["theta_scaled"], 1)
                        wait_apart(pool, (s["theta_scaled"], m + 1))
                        pool.tensor_scalar(turn[p % 2][:, :], turn[p % 2][:, :], -float(MAGIC), float(-TWO_PI),
                                           ALU.add, ALU.mult).then_inc(s["turns_done"], 1)
                    if t_in(T, 2, NTG + 2):
                        wait_apart(pool, (o_copied, PAIRS * (T - 2) + p + 1))
                        for i in range(2):
                            t = 2 * p + i
                            pool.indirect_dma_start(yg, bass.IndirectOffsetOnAxis(ap=oid[par][:, t:t + 1], axis=0),
                                                    ob[:, t * P:(t + 1) * P], None,
                                                    bounds_check=K * TOK - 1, oob_is_err=False).then_inc(o_scattered[p], 16)
                if t_in(T, 0, NTG):
                    wait_apart(pool, (xt_in[par], 64 * (T - par) + 128), *((o_scattered[p], 32 * (T - 1)) for p in range(PAIRS)))
                    pool.tensor_copy(oid[par][:, :], xt[par][:, :].rearrange("p (t w) -> p t w", w=ROW)[:, :, P].bitcast(I32)
                                     ).then_inc(s["idx_copied"], 1)
            tiles_loop(pool, tiles)

            def results(g, par):
                if t_in(g, 0, NG):
                    root(s["rms_var"], s["rms_done"], rs3[:, par * GRP:(par + 1) * GRP], sse[:, par * GRP:(par + 1) * GRP], g)
            results_loop(pool, results)


_INS = ["x", "ctx_1024", "L0_ffn_router_w", "L0_ffn_router_bias", "L0_ffn_bank_mag", "L0_ffn_bank_freq",
        "L0_ffn_bank_phase", "L0_ffn_bank_down", "L0_ffn_norm_w"]


def kernel(**inputs):
    import numpy as _np
    import concourse.bacc as _bacc
    from concourse import mybir as _mybir
    from concourse.bass_utils import run_bass_kernel_spmd as _run

    nc = _bacc.Bacc("TRN2", target_bir_lowering=False, num_devices=1)
    arrays, args = {}, []
    values = [(name, _np.ascontiguousarray(inputs[name])) for name in _INS]
    values += [("consts", constants()), ("rows_of", output_rows())]
    for name, a in values:
        arrays[f"in_{name}"] = a
        args.append(nc.dram_tensor(f"in_{name}", a.shape, _mybir.dt.from_np(a.dtype), kind="ExternalInput").ap())
    args.append(nc.dram_tensor("out_0", (B, P, P), _mybir.dt.float32, kind="ExternalOutput").ap())
    build(nc, *args)
    r = _run(nc, [arrays], core_ids=[0])
    return r.results[0]["out_0"]
```

```python
from contextlib import ExitStack

import numpy as np

import concourse.bass as bass
from concourse import mybir

F32 = mybir.dt.float32
BF16 = mybir.dt.bfloat16
I32 = mybir.dt.int32
U32 = mybir.dt.uint32
ALU = mybir.AluOpType
ACT = mybir.ActivationFunctionType
AX = mybir.AxisListType

P = 128
B = 32
HEADS = 16
HEAD = P // HEADS
JH = 4
GRP = 4
NG = B // GRP
E = 16
H = 256
K = 2
TOK = B * P
ROW = 132
REG = TOK + P
NULL_ROW = E * REG
NT = TOK * K // P + E
TG = 8
PAIRS = TG // 2
NTG = NT // TG
ZEROED = 8
DROP = 1 << 20
LN_EPS, RMS_EPS = 1e-5, 1e-6
TWO_PI = 2 * np.pi
MAGIC = 1.5 * 2.0 ** 23

C_CQ, C_SQ, C_CK, C_SK, C_CAUSAL, C_IDENT, C_BEFORE, C_ONES = (P * i for i in range(8))
C_IOTA = 8 * P
C_BASE = C_IOTA + E
C_TILE = C_BASE + E
C_END = C_TILE + NT


def constants():
    c = np.zeros((P, C_END), np.float64)
    pos = np.arange(P)[:, None]
    f = np.arange(P)[None, :]
    head, pair, odd = f // HEAD, (f % HEAD) // 2, f % 2
    gamma = 1.0 - np.exp(np.linspace(np.log(1.0 / 32.0), np.log(1.0 / 512.0), HEADS))[head]
    scale = ((2.0 * pair + 0.4 * HEAD) / (1.4 * HEAD)) ** (pos / 512.0)
    angle = pos / 10000.0 ** (pair / (HEAD // 2))
    sign = np.where(odd == 1, 1.0, -1.0)
    grow, shrink = scale * gamma ** pos, 1.0 / (scale * gamma ** pos)
    c[:, C_CQ:C_CQ + P] = np.cos(angle) * grow
    c[:, C_SQ:C_SQ + P] = np.sin(angle) * sign * grow
    c[:, C_CK:C_CK + P] = np.cos(angle) * shrink
    c[:, C_SK:C_SK + P] = (np.sin(angle) * sign * shrink)[:, np.arange(P) ^ 1]
    c[:, C_CAUSAL:C_CAUSAL + P] = f >= pos
    c[:, C_IDENT:C_IDENT + P] = f == pos
    c[:, C_BEFORE:C_BEFORE + P] = pos < f
    c[:, C_ONES:C_ONES + P] = 1.0
    c[:, C_IOTA:C_IOTA + E] = np.arange(E)
    c[:, C_BASE:C_BASE + E] = np.arange(E) * REG
    c[:, C_TILE:C_TILE + NT] = np.arange(NT)
    return c.astype(np.float32)


def output_rows():
    s, b, k = np.meshgrid(np.arange(P), np.arange(B), np.arange(K), indexing="ij")
    return np.ascontiguousarray((k * TOK + b * P + s).reshape(P, B * K).astype(np.int32))


def wait(eng, sem, value):
    if not isinstance(value, int) or value > 0:
        eng.wait_ge(sem, value)


def build(nc, x, ctx_in, router_w, router_bias, bank_mag, bank_freq, bank_phase, bank_down, norm_w,
          consts, rows_of, out):
    xg = nc.dram_tensor("routed_rows", (NULL_ROW + P, ROW), F32).ap()
    yg = nc.dram_tensor("expert_outputs", (K * TOK, P), F32).ap()
    x_v = x.rearrange("b s f -> s b f")
    ctx_v = ctx_in.rearrange("b s f -> s b f")
    out_v = out.rearrange("b s f -> s b f")
    yg_v = yg.rearrange("(k b s) f -> s k b f", k=K, b=B)

    with ExitStack() as st:
        def sb(name, cols, dt=F32, parts=P):
            return st.enter_context(nc.sbuf_tensor(name, [parts, cols], dt))

        def sem(name):
            return st.enter_context(nc.semaphore(name))

        cst = sb("cst", C_END)
        rowid = sb("rowid", B * K, I32)
        wmf = sb("wmf", E * 2 * H)
        wdn = sb("wdn", E * 2 * P)
        phase = sb("phase", E * H)
        xa = sb("xa", B * P)
        ca = sb("ca", B * P)
        rw = sb("rw", P, parts=E)
        rwT = sb("rwT", E)
        rbias = sb("rbias", E)
        nw = sb("nw", P)
        causal4 = sb("causal4", 4 * P)
        before_b = sb("before_b", P, BF16)
        ones_b = sb("ones_b", P, BF16)
        halfneg = sb("halfneg", 8)
        pad = sb("pad", ROW)
        st1, mv1, ve1, rstd1, shift1 = sb("st1", GRP * 6), sb("mv1", GRP * 2), sb("ve1", GRP), sb("rstd1", B), sb("shift1", B)
        st2, mv2, ve2, rstd2, shift2 = sb("st2", GRP * 6), sb("mv2", GRP * 2), sb("ve2", GRP), sb("rstd2", B), sb("shift2", B)
        xn = [sb(f"xn{i}", P) for i in range(2)]
        q1, q2, k1, k2 = (sb(n, P) for n in ("q1", "q2", "k1", "k2"))
        turned = sb("turned", 10 * 4 * P)
        qexp, kexp, vexp, qT, kT = ([turned[:, (2 * a + i) * 4 * P:(2 * a + i + 1) * 4 * P] for i in range(2)]
                                    for a in range(5))
        masked = sb("masked", 2 * HEADS * P)
        sm = [masked[:, i * HEADS * P:(i + 1) * HEADS * P] for i in range(2)]
        oT = sb("oT", P)
        xln = sb("xln", GRP * P)
        xlnT = sb("xlnT", GRP * P)
        rowb = sb("rowb", GRP * K * ROW)
        lg = sb("lg", GRP * E)
        mx8, mi8 = sb("mx8", GRP * 8), sb("mi8", GRP * 8, U32)
        ixf = sb("ixf", GRP * K)
        oh = sb("oh", GRP * K * E)
        msel = sb("msel", GRP * E, BF16)
        posb, prod, slf = sb("posb", GRP * E), sb("prod", GRP * K * E), sb("slf", GRP * K)
        sli = sb("sli", GRP * K, I32)
        msum, macc = sb("msum", E), sb("macc", E)
        macc_b = sb("macc_b", E, BF16)
        v12 = sb("v12", B * K)
        wk = sb("wk", K * B)
        wtmp = sb("wtmp", B)
        cnt, cnt_i, nt_i, ntf = sb("cnt", E), sb("cnt_i", E, I32), sb("nt_i", E, I32), sb("ntf", E)
        tend, zero16 = sb("tend", E), sb("zero16", E)
        fill_f, fill_i = sb("fill_f", E), sb("fill_i", E, I32)
        ge = sb("ge", NT * E)
        te, ts_, tb = sb("te", NT), sb("ts_", NT), sb("tb", NT)
        te_i, tb_i = sb("te_i", NT, I32), sb("tb_i", NT, I32)
        xt = [sb(f"xt{i}", TG * ROW) for i in range(2)]
        oid = [sb(f"oid{i}", TG, I32) for i in range(2)]
        xtT = [sb(f"xtT{i}", 2 * P) for i in range(2)]
        th, ex, rr = ([t[:, i * TG * H:(i + 1) * TG * H] for i in range(2)] for t in (turned, masked, ca))
        turn = [sb(f"turn{i}", 2 * H) for i in range(2)]
        hb = [sb(f"hb{i}", 2 * H) for i in range(2)]
        hT = [sb(f"hT{i}", 4 * P) for i in range(2)]
        ob = sb("ob", TG * P)
        o1, o2 = masked, ca
        ss, sse, rs3 = (sb(n, B) for n in ("ss", "sse", "rs3"))

        ps = st.enter_context(nc.psum_tensor("ps", [P, 8, 512], F32))
        S4 = [ps[:, g, :] for g in range(4)]
        PQ, PK = ps[:, 4, :], ps[:, 5, :]
        P_OT, P_X2 = ps[:, 6, 0:P], ps[:, 6, :]
        P_O, P_LG, P_POS, P_CNT = ps[:, 7, 0:P], ps[:, 7, P:P + GRP * E], ps[:, 7, 256:256 + GRP * E], ps[:, 7, 384:384 + E]

        P_XT, P_HT, P_DOWN = [ps[:, 4, 0:2 * P], ps[:, 7, 0:2 * P]], ps[:, 5, :], ps[:, 6, 0:2 * P]

        identity = cst[:, C_IDENT:C_IDENT + P]

        names = """waited consts_in x_in ctx_in w_in freq_in freq_scaled small_in phase_in tables_ready pow_ready zero_ready rw_turned rw_copied
            ln1_stats ln1_mv ln1_var ln1_rstd ln1_shift ln2_stats ln2_mv ln2_var ln2_rstd ln2_shift
            xn_done q_mul q_exp k_mul k_exp q_turned k_turned q_copied k_copied v_exp
            scores_done masked_done av_done ot_copied o_turned x2_done
            xln_done xln_turned xln_copied logits_done
            lg_done max_done maxi_done ixf_done oh_done sel_done pos_done posb_done prod_done slf_done slot_done
            row_copied row_id msum_done macc_done macc_copied rows_scattered v12_done
            cnt_done tab tab_ready wdiff wexp wk_done fills_done pad_ready
            phase_ready
            idx_copied xt_turned xt_copied mf_done abs_done relu_done tanh_done exp_done ln_done sin_done
            theta_sum turns_done theta_done hid_done h_turned h_copied down_done o_copied
            y1_done y2_done sq_done rms_var rms_done yn_done out_ready out_done""".split()
        s = {n: sem(n) for n in names}
        xt_in = [sem(f"xt_in{i}") for i in range(2)]
        o_scattered = [sem(f"o_scattered{i}") for i in range(PAIRS)]
        o12_in = [sem(f"o12_in{i}") for i in range(2)]

        def wait_apart(eng, *counts):
            for c, v in counts:
                if not isinstance(v, int) or v > 0:
                    eng.wait_ge(c, v)
                    eng.sem_inc(s["waited"], 1)

        def diag(t, outer, dims):
            return bass.AP(tensor=t.tensor, offset=t.offset, ap=[t.ap[0], [P + outer, 4]] + dims)

        def by_head(t):
            return diag(t, HEAD, [[32, 4], [1, HEAD]])

        def by_group_pairs(t):
            return diag(t, 32, [[2, 16], [1, 2]])

        def head_view(a):
            return a.rearrange("p (g j d) -> p j g d", g=4, j=JH)

        def group_pairs(a):
            return a.rearrange("p (g i two) -> p g i two", g=4, two=2)

        def swap(a):
            return a.rearrange("p (i two) -> p i two", two=2)[:, :, ::-1]

        def pairs(a):
            return a.rearrange("p (i two) -> p i two", two=2)

        def batch(t, n, width=P):
            return t[:, bass.ds(n * width, width)]

        def groups_loop(eng, body):
            body(0)
            body(1)
            with eng.Fori(2, NG - 1) as G:
                body(G)
            for G in range(NG - 1, NG + 2):
                body(G)

        def is_in(G, lo, hi):
            return not isinstance(G, int) or lo <= G < hi

        def tiles_loop(eng, body):
            for T in range(4):
                body(T, T % 2)
            with eng.Fori(2, NTG // 2) as u:
                body(u * 2, 0)
                body(u * 2 + 1, 1)
            body(NTG, 0)
            body(NTG + 1, 1)

        def table(eng, t, T, max_val):
            _, values = nc.values_load_multi_w_load_instructions(
                t[0:1, bass.ds(T * TG, TG)], engines=[eng.engine], min_val=0, max_val=max_val,
                skip_runtime_bounds_check_because="the table is made of sums of counts, and capped where it is written")
            return values

        def results_loop(eng, body):
            body(0, 0)
            body(1, 1)
            with eng.Fori(1, NG // 2) as u:
                body(u * 2, 0)
                body(u * 2 + 1, 1)
            body(NG, 0)
            body(NG + 1, 1)

        def t_in(T, lo, hi):
            return not isinstance(T, int) or lo <= T < hi

        block = st.enter_context(nc.Block())

        @block.sync
        def _(sp):
            sp.dma_start(cst[:, :], consts).then_inc(s["consts_in"], 16)
            sp.dma_start(rw[:, :], router_w).then_inc(s["small_in"], 16)
            sp.dma_start(rbias[:, :], router_bias.rearrange("(o e) -> o e", o=1).to_broadcast([P, E])).then_inc(s["small_in"], 16)
            sp.dma_start(nw[:, :], norm_w.rearrange("(o f) -> o f", o=1).to_broadcast([P, P])).then_inc(s["small_in"], 16)
            sp.dma_start(rowid[:, :], rows_of).then_inc(s["small_in"], 16)
            with sp.Fori(0, NG) as g:
                sp.dma_start(batch(xa, g, GRP * P).rearrange("p (b f) -> p b f", b=GRP),
                             x_v[:, bass.ds(g * GRP, GRP), :]).then_inc(s["x_in"], 16)
                sp.dma_start(batch(ca, g, GRP * P).rearrange("p (b f) -> p b f", b=GRP),
                             ctx_v[:, bass.ds(g * GRP, GRP), :]).then_inc(s["ctx_in"], 16)
                wait_apart(sp, (s["x_in"], 16 * g + 16), (s["ctx_in"], 16 * g + 16))
            wmf_v = wmf[:, :].rearrange("d (e m h) -> d e m h", e=E, m=2)
            sp.dma_start(wmf_v[:, :, 0, :], bank_mag.rearrange("e d h -> d e h")).then_inc(s["w_in"], 16)
            sp.dma_start(wmf_v[:, :, 1, :], bank_freq.rearrange("e d h -> d e h")).then_inc(s["freq_in"], 16)
            sp.dma_start(wdn[:, :].rearrange("p (e c d) -> p e c d", e=E, c=2),
                         bank_down.rearrange("e (c p) d -> p e c d", c=2)).then_inc(s["w_in"], 16)
            sp.dma_start(phase[:, :], bank_phase.rearrange("(o e) h -> o (e h)", o=1).to_broadcast([P, E * H])).then_inc(s["phase_in"], 16)

            sp.wait_ge(s["pad_ready"], 2)
            sp.dma_start(xg[NULL_ROW:NULL_ROW + P, :], pad[:, :]).then_inc(s["fills_done"], 16)
            sp.wait_ge(s["tab"], 3)
            with sp.Fori(0, E // TG) as half:
                for row in table(sp, fill_i, half, NULL_ROW - P):
                    sp.dma_start(xg[bass.ds(row, P), :], pad[:, :]).then_inc(s["fills_done"], 16)
            sp.wait_ge(s["tab_ready"], 1)
            sp.wait_ge(s["fills_done"], 16 * (E + 1))
            sp.wait_ge(s["rows_scattered"], 16 * GRP * K * NG)

            def tiles(T, par):
                if not t_in(T, 0, NTG):
                    return
                wait_apart(sp, (s["idx_copied"], T - 1), (s["xt_turned"], PAIRS * (T - 1)))
                for i, base in enumerate(table(sp, tb_i, T, NULL_ROW)):
                    sp.dma_start(xt[par][:, i * ROW:(i + 1) * ROW], xg[bass.ds(base, P), :]).then_inc(xt_in[par], 16)
            tiles_loop(sp, tiles)

            for p in range(PAIRS):
                sp.wait_ge(o_scattered[p], 32 * NTG)

            def load_outputs(g, par):
                if not t_in(g, 0, NG):
                    return
                wait_apart(sp, (o12_in[par], 16 * (g - par)))
                for k, o in enumerate((o1, o2)):
                    sp.dma_start(batch(o, g, GRP * P).rearrange("p (b f) -> p b f", b=GRP),
                                 yg_v[:, k, bass.ds(g * GRP, GRP), :]).then_inc(o12_in[par], 16)
            results_loop(sp, load_outputs)

            with sp.Fori(0, NG) as g:
                wait_apart(sp, (s["out_ready"], g + 1))
                sp.dma_start(out_v[:, bass.ds(g * GRP, GRP), :],
                             batch(o1, g, GRP * P).rearrange("p (b f) -> p b f", b=GRP)).then_inc(s["out_done"], 16)
            sp.wait_ge(s["out_done"], 16 * NG)

        @block.tensor
        def _(pe):
            pe.wait_ge(s["consts_in"], 16)
            pe.wait_ge(s["small_in"], 64)
            pe.transpose(P_LG[:, 0:E], rw[:, :], identity[0:E, 0:E]).then_inc(s["rw_turned"], 1)

            def turn_qk(m, par):
                pe.wait_ge(s["q_exp"], m + 1)
                wait(pe, s["q_copied"], m)
                for j in range(4):
                    mm = pe.transpose(PQ[:, j * P:(j + 1) * P], qexp[par][:, j * P:(j + 1) * P], identity)
                mm.then_inc(s["q_turned"], 1)
                pe.wait_ge(s["k_exp"], m + 1)
                wait(pe, s["k_copied"], m)
                for g in range(4):
                    mm = pe.transpose(PK[:, g * P:(g + 1) * P], kexp[par][:, g * P:(g + 1) * P], identity)
                mm.then_inc(s["k_turned"], 1)

            def scores(n, par):
                pe.wait_ge(s["q_copied"], n + 1)
                pe.wait_ge(s["k_copied"], n + 1)
                for g in range(4):
                    wait(pe, s["masked_done"], 4 * n + g - 3)
                    pe.matmul(S4[g], kT[par][:, g * P:(g + 1) * P], qT[par][:, :],
                              start=True, stop=True).then_inc(s["scores_done"], 1)

            def values(n, par, turned_groups):
                pe.wait_ge(s["masked_done"], 4 * n + 4)
                pe.wait_ge(s["v_exp"], n + 1)
                wait(pe, s["ot_copied"], n)
                wait(pe, s["xln_copied"], turned_groups)
                for j in range(JH):
                    for g in range(4):
                        mm = pe.matmul(P_OT[32 * g:32 * g + 32, :], vexp[par][:, j * P + 32 * g:j * P + 32 * g + 32],
                                       sm[par][:, (4 * g + j) * P:(4 * g + j + 1) * P],
                                       start=(j == 0), stop=(j == JH - 1))
                mm.then_inc(s["av_done"], 1)

            def turn_o(n, lg_groups, pos_groups):
                pe.wait_ge(s["ot_copied"], n + 1)
                wait(pe, s["x2_done"], n)
                wait(pe, s["lg_done"], lg_groups)
                wait(pe, s["posb_done"], pos_groups)
                pe.transpose(P_O, oT[:, :], identity).then_inc(s["o_turned"], 1)

            def turn_xln(R):
                pe.wait_ge(s["xln_done"], GRP * R + GRP)
                wait(pe, s["ot_copied"], GRP * R + 6 if not isinstance(R, int) else min(GRP * R + 6, B))
                for b in range(GRP):
                    mm = pe.transpose(P_X2[:, b * P:(b + 1) * P], xln[:, b * P:(b + 1) * P], identity)
                mm.then_inc(s["xln_turned"], 1)

            def logits(R):
                pe.wait_ge(s["xln_copied"], R + 1)
                pe.wait_ge(s["x2_done"], GRP * R + 6 if not isinstance(R, int) else min(GRP * R + 6, B))
                for b in range(GRP):
                    mm = pe.matmul(P_LG[:, b * E:(b + 1) * E], xlnT[:, b * P:(b + 1) * P], rwT[:, :], start=True, stop=True)
                mm.then_inc(s["logits_done"], 1)

            def positions(R):
                pe.wait_ge(s["sel_done"], R + 1)
                pe.wait_ge(s["macc_copied"], R + 1)
                pe.wait_ge(s["x2_done"], GRP * R + 8 if not isinstance(R, int) else min(GRP * R + 8, B))
                pe.matmul(P_POS, before_b[:, :], msel[:, :], start=True, stop=False)
                for b in range(GRP - 1):
                    pe.matmul(P_POS[:, (b + 1) * E:].rearrange("p (b e) -> p b e", e=E), ones_b[:, :],
                              msel[:, b * E:(b + 1) * E].unsqueeze(1).to_broadcast([P, GRP - 1 - b, E]), start=False, stop=False)
                pe.matmul(P_POS.rearrange("p (b e) -> p b e", e=E), ones_b[:, :],
                          macc_b[:, :].unsqueeze(1).to_broadcast([P, GRP, E]), start=False, stop=True).then_inc(s["pos_done"], 1)

            pe.wait_ge(s["rw_copied"], 1)
            turn_qk(0, 0)

            def body(G):
                for i in range(GRP):
                    n = GRP * G + i
                    if is_in(G, 0, NG):
                        scores(n, i % 2)
                    if i == 3 and is_in(G, 1, NG + 1):
                        turn_xln(G - 1)
                    if is_in(G, 0, NG) and not (isinstance(G, int) and n + 1 >= B):
                        turn_qk(n + 1, (i + 1) % 2)
                    if not isinstance(G, int) or 0 <= n - 2 < B:
                        turn_o(n - 2, G - 1, G - 1 if i >= 2 else G - 2)
                    if not isinstance(G, int) or 0 <= n - 1 < B:
                        values(n - 1, (i + 1) % 2, G if i == 3 else G - 1)
                    if i == 3 and is_in(G, 1, NG + 1):
                        logits(G - 1)
                    if i == 1 and is_in(G, 2, NG + 2):
                        positions(G - 2)
            groups_loop(pe, body)

            pe.wait_ge(s["macc_copied"], NG + 1)
            pe.matmul(P_CNT, ones_b[:, :], macc_b[:, :], start=True, stop=True).then_inc(s["cnt_done"], 1)

            pe.wait_ge(s["w_in"], 32)
            pe.wait_ge(s["freq_scaled"], 1)
            pe.wait_ge(s["tab_ready"], 1)

            def turn_x(T, par, p):
                m = PAIRS * T + p
                wait(pe, s["xt_copied"], m - 1)
                for i in range(2):
                    t = 2 * p + i
                    mm = pe.transpose(P_XT[p % 2][:, i * P:(i + 1) * P], xt[par][:, t * ROW:t * ROW + P], identity)
                mm.then_inc(s["xt_turned"], 1)

            def turn_h(m, q):
                pe.wait_ge(s["hid_done"], m + 1)
                wait(pe, s["h_copied"], m)
                for c in range(4):
                    mm = pe.transpose(P_HT[:, c * P:(c + 1) * P], hb[q][:, c * P:(c + 1) * P], identity)
                mm.then_inc(s["h_turned"], 1)

            def mag_freq(m, q, experts):
                wait(pe, s["tanh_done"], m - 1)
                wait(pe, s["abs_done"], m - 1)
                wait(pe, s["relu_done"], 2 * (m - 1))
                pe.wait_ge(s["xt_copied"], m + 1)
                for i, e in enumerate(experts):
                    for c in range(2):
                        mm = pe.matmul(ps[:, 2 * q + c, i * H:(i + 1) * H], xtT[q][:, i * P:(i + 1) * P],
                                       wmf[:, bass.ds(e * (2 * H) + c * H, H)], start=True, stop=True)
                mm.then_inc(s["mf_done"], 1)

            def down(m, q, experts):
                pe.wait_ge(s["h_copied"], m + 1)
                wait(pe, s["o_copied"], m)
                for i, e in enumerate(experts):
                    for c in range(2):
                        mm = pe.matmul(P_DOWN[:, i * P:(i + 1) * P], hT[q][:, (2 * i + c) * P:(2 * i + c + 1) * P],
                                       wdn[:, bass.ds(e * (2 * P) + c * P, P)], start=(c == 0), stop=(c == 1))
                mm.then_inc(s["down_done"], 1)

            def tiles(T, par):
                first, last = t_in(T, 0, NTG), t_in(T, 2, NTG + 2)
                if first:
                    new = table(pe, te_i, T, E - 1)
                    pe.wait_ge(xt_in[par], 64 * (T - par) + 128)
                    turn_x(T, par, 0)
                for p in range(PAIRS):
                    q = p % 2
                    if first and p + 1 < PAIRS:
                        turn_x(T, par, p + 1)
                    if first:
                        mag_freq(PAIRS * T + p, q, new[2 * p:2 * p + 2])
                    if last and p == 0:
                        old = table(pe, te_i, T - 2, E - 1)
                    if last:
                        turn_h(PAIRS * (T - 2) + p, q)
                        if p:
                            down(PAIRS * (T - 2) + p - 1, 1 - q, old[2 * p - 2:2 * p])
                if last:
                    down(PAIRS * (T - 2) + PAIRS - 1, (PAIRS - 1) % 2, old[TG - 2:])
            tiles_loop(pe, tiles)

        @block.scalar
        def _(act):
            act.wait_ge(s["rw_turned"], 1)
            act.copy(rwT[:, :], P_LG[:, 0:E]).then_inc(s["rw_copied"], 1)

            def take_qk(m, par):
                act.wait_ge(s["q_turned"], m + 1)
                wait(act, s["scores_done"], 4 * (m - 1))
                act.copy(qT[par][:, :], PQ).then_inc(s["q_copied"], 1)
                act.wait_ge(s["k_turned"], m + 1)
                act.copy(kT[par][:, :], PK).then_inc(s["k_copied"], 1)

            def expand_v(m, g, par):
                act.wait_ge(s["ctx_in"], 16 * g + 16)
                wait(act, s["av_done"], m - 1)
                act.copy(by_head(vexp[par]), head_view(batch(ca, m))).then_inc(s["v_exp"], 1)

            def normalise_q(m, g, i):
                if i == 0:
                    act.wait_ge(s["ln1_shift"], g + 1)
                wait(act, s["q_mul"], 2 * (m - 1))
                act.activation(xn[i % 2][:, :], batch(xa, m), ACT.Identity, scale=rstd1[:, bass.ds(m, 1)],
                               bias=shift1[:, bass.ds(m, 1)]).then_inc(s["xn_done"], 1)

            def normalise(R):
                act.wait_ge(s["ln2_shift"], R + 1)
                wait(act, s["row_copied"], K * R)
                for b in range(GRP):
                    n = GRP * R + b
                    act.activation(xln[:, b * P:(b + 1) * P], batch(xa, n), ACT.Identity, scale=rstd2[:, bass.ds(n, 1)],
                                   bias=shift2[:, bass.ds(n, 1)]).then_inc(s["xln_done"], 1)

            def copy_rows(R):
                wait(act, s["rows_scattered"], 16 * GRP * K * R)
                act.wait_ge(s["xln_done"], GRP * R + GRP)
                rows = rowb[:, :].rearrange("p (b k w) -> p b k w", b=GRP, k=K)
                for k in range(K):
                    act.copy(rows[:, :, k, 0:P], xln[:, :].rearrange("p (b f) -> p b f", b=GRP)).then_inc(s["row_copied"], 1)

            act.wait_ge(s["zero_ready"], ZEROED)
            for i in range(2):
                normalise_q(i, 0, i)
            take_qk(0, 0)
            expand_v(0, 0, 0)

            def body(G):
                for i in range(GRP):
                    n = GRP * G + i
                    more = is_in(G, 0, NG) and not (isinstance(G, int) and n + 1 >= B)
                    if is_in(G, 0, NG) and not (isinstance(G, int) and n + 2 >= B):
                        normalise_q(n + 2, G + (i + 2) // GRP, (i + 2) % GRP)
                    if i == 1 and is_in(G, 2, NG + 2):
                        copy_rows(G - 2)
                    if more:
                        take_qk(n + 1, (i + 1) % 2)
                    if i == 3 and is_in(G, 1, NG + 1):
                        act.wait_ge(s["xln_turned"], G)
                        wait(act, s["logits_done"], G - 1)
                        act.copy(xlnT[:, :], P_X2).then_inc(s["xln_copied"], 1)
                    if not isinstance(G, int) or 0 <= n - 1 < B:
                        act.wait_ge(s["av_done"], n)
                        wait(act, s["o_turned"], n - 1)
                        act.copy(oT[:, :], P_OT).then_inc(s["ot_copied"], 1)
                    if more:
                        expand_v(n + 1, G + (i + 1) // GRP, (i + 1) % 2)
                    if i == 2 and is_in(G, 1, NG + 1):
                        normalise(G - 1)
            groups_loop(act, body)

            act.wait_ge(s["freq_in"], 16)
            freqs = wmf[:, :].rearrange("d (e m h) -> d e m h", e=E, m=2)[:, :, 1, :]
            act.activation(freqs, freqs, ACT.Copy, scale=float(1 / TWO_PI)).then_inc(s["freq_scaled"], 1)
            act.wait_ge(s["phase_in"], 16)
            act.activation(phase[:, :], phase[:, :], ACT.Copy, scale=float(1 / TWO_PI),
                           bias=float((0.1 + np.pi / 2) / TWO_PI)).then_inc(s["phase_ready"], 1)

            act.wait_ge(s["wdiff"], 1)
            act.activation(wtmp[:, :], wtmp[:, :], ACT.Exp).then_inc(s["wexp"], 1)

            def sine(T, par, p):
                m = PAIRS * T + p
                cols = slice(p * 2 * H, (p + 1) * 2 * H)
                act.wait_ge(s["theta_done"], m + 1)
                act.activation(rr[par][:, cols], rr[par][:, cols], ACT.Sin, scale=float(-TWO_PI)).then_inc(s["sin_done"], 1)

            def take_outputs(T, p):
                act.wait_ge(s["down_done"], PAIRS * T + p + 1)
                wait(act, o_scattered[p], 32 * T)
                act.copy(ob[:, 2 * p * P:(2 * p + 2) * P], P_DOWN).then_inc(s["o_copied"], 1)

            def tiles(T, par):
                act.preload_act_table_set("silu_and_others")
                for p in range(PAIRS):
                    q = p % 2
                    if p >= 2 and t_in(T, 1, NTG + 1):
                        sine(T - 1, 1 - par, p - 2)
                    if p < 2 and t_in(T, 2, NTG + 2):
                        sine(T - 2, par, p + 2)
                    if t_in(T, 2, NTG + 2):
                        act.wait_ge(s["h_turned"], PAIRS * (T - 2) + p + 1)
                        wait(act, s["down_done"], PAIRS * (T - 2) + p - 1)
                        act.copy(hT[q][:, :], P_HT).then_inc(s["h_copied"], 1)
                    if t_in(T, 0, NTG):
                        act.wait_ge(s["mf_done"], PAIRS * T + p + 1)
                        wait(act, s["hid_done"], PAIRS * (T - 2) + p + 1)
                        act.activation(th[par][:, p * 2 * H:(p + 1) * 2 * H], ps[:, 2 * q, :], ACT.Tanh).then_inc(s["tanh_done"], 1)
                    if p and t_in(T, 2, NTG + 2):
                        take_outputs(T - 2, p - 1)
                if t_in(T, 0, NTG):
                    act.preload_act_table_set("natural_log_exp_and_others")
                    act.wait_ge(s["abs_done"], PAIRS * T + PAIRS)
                    act.activation(ex[par][:, :], ex[par][:, :], ACT.Exp, scale=float(-TWO_PI)).then_inc(s["exp_done"], 1)
                    act.wait_ge(s["exp_done"], T + 1)
                    act.activation(ex[par][:, :], ex[par][:, :], ACT.Ln, bias=1.0).then_inc(s["ln_done"], 1)
                if t_in(T, 2, NTG + 2):
                    take_outputs(T - 2, PAIRS - 1)
            tiles_loop(act, tiles)

            act.wait_ge(s["wk_done"], 1)

            def results(g, par):
                if t_in(g, 0, NG):
                    act.wait_ge(o12_in[par], 16 * (g - par) + 32)
                    for b in range(GRP):
                        n = g * GRP + b
                        act.activation(batch(o1, n), batch(o1, n), ACT.Copy, scale=wk[:, bass.ds(n, 1)]).then_inc(s["y1_done"], 1)
                if t_in(g, 1, NG + 1):
                    for b in range(GRP):
                        n = (g - 1) * GRP + b
                        act.wait_ge(s["y2_done"], n + 1)
                        act.activation(batch(o2, n), batch(o1, n), ACT.Square,
                                       accum_out=ss[:, bass.ds(n, 1)]).then_inc(s["sq_done"], 1)
            results_loop(act, results)

        @block.vector
        def _(dve):
            for t in qexp:
                dve.memset(t[:, :], 0.0).then_inc(s["zero_ready"], 1)
            dve.memset(rowb[:, :], 0.0).then_inc(s["zero_ready"], 1)
            dve.memset(macc[:, :], 0.0).then_inc(s["macc_done"], 1)
            dve.memset(macc_b[:, :], 0.0).then_inc(s["macc_copied"], 1)
            dve.memset(zero16[:, :], 0.0).then_inc(s["zero_ready"], 1)
            dve.memset(pad[:, 0:P], 0.0).then_inc(s["pad_ready"], 1)
            dve.memset(pad[:, P:ROW].bitcast(I32), DROP).then_inc(s["pad_ready"], 1)
            dve.wait_ge(s["consts_in"], 16)
            dve.tensor_copy(causal4[:, :].rearrange("p (j s) -> p j s", j=4),
                            cst[:, C_CAUSAL:C_CAUSAL + P].unsqueeze(1).to_broadcast([P, 4, P])).then_inc(s["tables_ready"], 1)
            dve.tensor_copy(before_b[:, :], cst[:, C_BEFORE:C_BEFORE + P]).then_inc(s["tables_ready"], 1)
            dve.tensor_copy(ones_b[:, :], cst[:, C_ONES:C_ONES + P]).then_inc(s["tables_ready"], 1)

            def stats(xs, stt_, mv, ve, names, count):
                for b in range(GRP):
                    dve.bn_stats(stt_[:, 6 * b:6 * b + 6], xs(b)).then_inc(s[names[0]], 1)
                for b in range(GRP):
                    wait_apart(dve, (s[names[0]], GRP * count + b + 1))
                    dve.bn_aggr(mv[:, 2 * b:2 * b + 2], stt_[:, 6 * b:6 * b + 6]).then_inc(s[names[1]], 1)
                dve.wait_ge(s[names[1]], GRP * count + GRP)
                dve.tensor_scalar(ve[:, :], mv[:, 1:2 * GRP:2], LN_EPS, None, ALU.add).then_inc(s[names[2]], 1)

            def stats1(g):
                dve.wait_ge(s["x_in"], 16 * g + 16)
                stats(lambda b: batch(xa, GRP * g + b), st1, mv1, ve1, ["ln1_stats", "ln1_mv", "ln1_var"], g)

            def shift(mv, rstd, rstd_sem, shifts, shift_sem, g):
                dve.wait_ge(rstd_sem, g + 1)
                dve.scalar_tensor_tensor(out=batch(shifts, g, GRP), in0=mv[:, 0:2 * GRP:2], scalar=-1.0,
                                         in1=batch(rstd, g, GRP), op0=ALU.mult, op1=ALU.mult).then_inc(shift_sem, 1)

            def shift_1(g):
                shift(mv1, rstd1, s["ln1_rstd"], shift1, s["ln1_shift"], g)

            def shift_2(g):
                shift(mv2, rstd2, s["ln2_rstd"], shift2, s["ln2_shift"], g)

            def rotate_q(m, i):
                wait(dve, s["q_exp"], m)
                dve.wait_ge(s["xn_done"], m + 1)
                dve.tensor_tensor(q1[:, :], xn[i % 2][:, :], cst[:, C_CQ:C_CQ + P], ALU.mult).then_inc(s["q_mul"], 1)
                dve.tensor_tensor(pairs(q2[:, :]), swap(xn[i % 2][:, :]), pairs(cst[:, C_SQ:C_SQ + P]), ALU.mult).then_inc(s["q_mul"], 1)
                dve.wait_ge(s["q_mul"], 2 * m + 2)
                wait(dve, s["q_turned"], m - 1)
                dve.tensor_tensor(by_head(qexp[i % 2]), head_view(q1[:, :]), head_view(q2[:, :]), ALU.add).then_inc(s["q_exp"], 1)

            stats1(0)
            shift_1(0)
            dve.wait_ge(s["zero_ready"], ZEROED)
            for i in range(2):
                rotate_q(i, i)

            def mask(n, par):
                wait(dve, s["av_done"], n - 1)
                for g in range(4):
                    dve.wait_ge(s["scores_done"], 4 * n + g + 1)
                    dve.tensor_tensor(sm[par][:, g * 4 * P:(g + 1) * 4 * P], S4[g], causal4[:, :],
                                      ALU.mult).then_inc(s["masked_done"], 1)

            def add_attention(n):
                dve.wait_ge(s["o_turned"], n + 1)
                dve.tensor_tensor(batch(xa, n), batch(xa, n), P_O, ALU.add).then_inc(s["x2_done"], 1)

            def stats2(R):
                dve.wait_ge(s["x2_done"], GRP * R + GRP)
                stats(lambda b: batch(xa, GRP * R + b), st2, mv2, ve2, ["ln2_stats", "ln2_mv", "ln2_var"], R)

            lg3 = lg[:, :].rearrange("p (b e) -> p b e", b=GRP)
            oh4 = oh[:, :].rearrange("p (b k e) -> p b k e", b=GRP, k=K)
            msel3 = msel[:, :].rearrange("p (b e) -> p b e", b=GRP)
            posb3 = posb[:, :].rearrange("p (b e) -> p b e", b=GRP)
            mx3 = mx8[:, :].rearrange("p (b r) -> p b r", b=GRP)
            mi3 = mi8[:, :].rearrange("p (b r) -> p b r", b=GRP)
            iota = cst[:, C_IOTA:C_IOTA + E].unsqueeze(1).unsqueeze(1)
            base = cst[:, C_BASE:C_BASE + E].unsqueeze(1)

            def take_logits(R):
                dve.wait_ge(s["logits_done"], R + 1)
                dve.tensor_tensor(lg3, P_LG.rearrange("p (b e) -> p b e", b=GRP),
                                  rbias[:, :].unsqueeze(1).to_broadcast([P, GRP, E]), ALU.add).then_inc(s["lg_done"], 1)

            def choose(R):
                wait_apart(dve, (s["lg_done"], R + 1))
                for b in range(GRP):
                    dve.max(mx3[:, b, :], lg3[:, b, :]).then_inc(s["max_done"], 1)
                for b in range(GRP):
                    wait_apart(dve, (s["max_done"], GRP * R + b + 1))
                    dve.max_index(mi3[:, b, :], mx3[:, b, :], lg3[:, b, :]).then_inc(s["maxi_done"], 1)
                dve.wait_ge(s["maxi_done"], GRP * R + GRP)
                dve.tensor_copy(ixf[:, :].rearrange("p (b k) -> p b k", k=K), mi3[:, :, 0:K]).then_inc(s["ixf_done"], 1)
                dve.tensor_copy(batch(v12, R, GRP * K).rearrange("p (b k) -> p b k", k=K), mx3[:, :, 0:K]).then_inc(s["v12_done"], 1)
                dve.wait_ge(s["ixf_done"], R + 1)
                dve.tensor_tensor(oh4, iota.to_broadcast([P, GRP, K, E]),
                                  ixf[:, :].rearrange("p (b k) -> p b k", k=K).unsqueeze(3).to_broadcast([P, GRP, K, E]),
                                  ALU.is_equal).then_inc(s["oh_done"], 1)
                dve.wait_ge(s["oh_done"], R + 1)
                dve.tensor_tensor(msel3, oh4[:, :, 0, :], oh4[:, :, 1, :], ALU.add).then_inc(s["sel_done"], 1)

            def take_positions(R):
                dve.wait_ge(s["pos_done"], R + 1)
                dve.tensor_tensor(posb3, P_POS.rearrange("p (b e) -> p b e", b=GRP), base.to_broadcast([P, GRP, E]),
                                  ALU.add).then_inc(s["posb_done"], 1)

            def place(R):
                dve.tensor_reduce(msum[:, :], msel3.rearrange("p b e -> p e b"), AX.X, ALU.add).then_inc(s["msum_done"], 1)
                dve.wait_ge(s["posb_done"], R + 1)
                dve.tensor_tensor(prod[:, :].rearrange("p (b k e) -> p b k e", b=GRP, k=K), oh4,
                                  posb3.unsqueeze(2).to_broadcast([P, GRP, K, E]), ALU.mult).then_inc(s["prod_done"], 1)
                dve.wait_ge(s["msum_done"], R + 1)
                dve.wait_ge(s["macc_done"], R + 1)
                dve.tensor_tensor(macc[:, :], macc[:, :], msum[:, :], ALU.add).then_inc(s["macc_done"], 1)
                dve.wait_ge(s["prod_done"], R + 1)
                dve.tensor_reduce(slf[:, :], prod[:, :].rearrange("p (c e) -> p c e", e=E), AX.X, ALU.add).then_inc(s["slf_done"], 1)
                dve.wait_ge(s["macc_done"], R + 2)
                dve.tensor_copy(macc_b[:, :], macc[:, :]).then_inc(s["macc_copied"], 1)
                dve.wait_ge(s["slf_done"], R + 1)
                wait(dve, s["rows_scattered"], 16 * GRP * K * R)
                dve.tensor_copy(sli[:, :], slf[:, :]).then_inc(s["slot_done"], 1)
                dve.tensor_copy(rowb[:, :].rearrange("p (c w) -> p c w", w=ROW)[:, :, P].bitcast(I32),
                                batch(rowid, R, GRP * K)).then_inc(s["row_id"], 1)

            def body(G):
                for i in range(GRP):
                    n = GRP * G + i
                    if i == 0 and is_in(G, 2, NG + 2):
                        take_logits(G - 2)
                    if i == 2 and is_in(G, 2, NG + 2):
                        take_positions(G - 2)
                    if i == 2 and is_in(G, 0, NG - 1):
                        shift_1(G + 1)
                    if is_in(G, 0, NG):
                        mask(n, i % 2)
                        if not (isinstance(G, int) and n + 2 >= B):
                            rotate_q(n + 2, i)
                    if i == 2 and is_in(G, 1, NG + 1):
                        shift_2(G - 1)
                    if not isinstance(G, int) or 0 <= n - 2 < B:
                        add_attention(n - 2)
                    if i == 0 and is_in(G, 2, NG + 2):
                        choose(G - 2)
                    if i == 1:
                        if is_in(G, 0, NG - 1):
                            stats1(G + 1)
                        if is_in(G, 1, NG + 1):
                            stats2(G - 1)
                    if i == 2 and is_in(G, 2, NG + 2):
                        place(G - 2)
            groups_loop(dve, body)

            done = [0]

            def step(ins):
                done[0] += 1
                ins.then_inc(s["tab"], 1)
                dve.wait_ge(s["tab"], done[0])
            dve.wait_ge(s["cnt_done"], 1)
            step(dve.tensor_copy(cnt[:, :], P_CNT))
            step(dve.tensor_tensor(fill_f[:, :], cnt[:, :], cst[:, C_BASE:C_BASE + E], ALU.add))
            step(dve.tensor_copy(fill_i[:, :], fill_f[:, :]))
            step(dve.tensor_scalar(cnt[:, :], cnt[:, :], float(P - 1), None, ALU.add))
            step(dve.tensor_copy(cnt_i[:, :], cnt[:, :]))
            step(dve.tensor_scalar(nt_i[:, :], cnt_i[:, :], 7, None, ALU.logical_shift_right))
            step(dve.tensor_copy(ntf[:, :], nt_i[:, :]))
            step(dve.tensor_tensor_scan(tend[:, :], ntf[:, :], zero16[:, :], 0.0, ALU.add, ALU.add))
            g1 = ge[0:1, :].rearrange("o (t e) -> o t e", e=E)
            step(dve.tensor_tensor(g1, cst[0:1, C_TILE:C_TILE + NT].unsqueeze(2).to_broadcast([1, NT, E]),
                                   tend[0:1, :].unsqueeze(1).to_broadcast([1, NT, E]), ALU.is_ge))
            step(dve.tensor_reduce(te[0:1, :], g1, AX.X, ALU.add))
            step(dve.tensor_tensor(g1, g1, ntf[0:1, :].unsqueeze(1).to_broadcast([1, NT, E]), ALU.mult))
            step(dve.tensor_reduce(ts_[0:1, :], g1, AX.X, ALU.add))
            step(dve.tensor_tensor(ts_[0:1, :], cst[0:1, C_TILE:C_TILE + NT], ts_[0:1, :], ALU.subtract))
            step(dve.tensor_scalar(ts_[0:1, :], ts_[0:1, :], float(P), None, ALU.mult))
            step(dve.scalar_tensor_tensor(out=tb[0:1, :], in0=te[0:1, :], scalar=float(REG), in1=ts_[0:1, :],
                                          op0=ALU.mult, op1=ALU.add))
            step(dve.tensor_scalar(tb[0:1, :], tb[0:1, :], float(NULL_ROW), None, ALU.min))
            step(dve.tensor_copy(tb_i[0:1, :], tb[0:1, :]))
            step(dve.tensor_scalar(te[0:1, :], te[0:1, :], float(E - 1), None, ALU.min))
            dve.tensor_copy(te_i[0:1, :], te[0:1, :]).then_inc(s["tab_ready"], 1)

            v3 = v12[:, :].rearrange("p (b k) -> p b k", k=K)
            dve.wait_ge(s["v12_done"], NG)
            dve.tensor_tensor(wtmp[:, :], v3[:, :, 1], v3[:, :, 0], ALU.subtract).then_inc(s["wdiff"], 1)
            dve.wait_ge(s["wexp"], 1)
            step(dve.tensor_scalar(wk[:, B:2 * B], wtmp[:, :], 1.0, None, ALU.add))
            step(dve.reciprocal(wk[:, 0:B], wk[:, B:2 * B]))
            dve.tensor_tensor(wk[:, B:2 * B], wtmp[:, :], wk[:, 0:B], ALU.mult).then_inc(s["wk_done"], 1)

            dve.wait_ge(s["phase_ready"], 1)
            dve.wait_ge(s["tab_ready"], 1)

            def hidden(m, par, p):
                cols = slice(p * 2 * H, (p + 1) * 2 * H)
                dve.wait_ge(s["sin_done"], m + 1)
                wait(dve, s["h_turned"], m - 1)
                dve.tensor_tensor(hb[p % 2][:, :], th[par][:, cols], rr[par][:, cols], ALU.mult).then_inc(s["hid_done"], 1)

            def whole_turns_off(T, par, p):
                cols = slice(p * 2 * H, (p + 1) * 2 * H)
                dve.wait_ge(s["turns_done"], PAIRS * T + p + 1)
                dve.scalar_tensor_tensor(out=rr[par][:, cols], in0=turn[p % 2][:, :], scalar=-float(MAGIC),
                                         in1=rr[par][:, cols], op0=ALU.add,
                                         op1=ALU.subtract).then_inc(s["theta_done"], 1)

            def take_x(m, q):
                dve.wait_ge(s["xt_turned"], m + 1)
                wait(dve, s["mf_done"], m - 1)
                dve.tensor_copy(xtT[q][:, :], P_XT[q]).then_inc(s["xt_copied"], 1)

            def tiles(T, par):
                first, middle, last = t_in(T, 0, NTG), t_in(T, 1, NTG + 1), t_in(T, 2, NTG + 2)
                if first:
                    experts = table(dve, te_i, T, E - 1)
                    take_x(PAIRS * T, 0)
                if last:
                    hidden(PAIRS * (T - 2), par, 0)
                for p in range(PAIRS):
                    q = p % 2
                    cols = slice(p * 2 * H, (p + 1) * 2 * H)
                    if first and p + 1 < PAIRS:
                        take_x(PAIRS * T + p + 1, 1 - q)
                    if last and p + 1 < PAIRS:
                        hidden(PAIRS * (T - 2) + p + 1, par, p + 1)
                    if first:
                        dve.wait_ge(s["mf_done"], PAIRS * T + p + 1)
                        freq = ps[:, 2 * q + 1, :]
                        dve.tensor_scalar(ex[par][:, cols].bitcast(I32), freq.bitcast(I32),
                                          0x7FFFFFFF, None, ALU.bitwise_and).then_inc(s["abs_done"], 1)
                        wait(dve, s["hid_done"], PAIRS * (T - 2) + p + 1)
                        for i in range(2):
                            e = experts[2 * p + i]
                            dve.scalar_tensor_tensor(out=rr[par][:, (2 * p + i) * H:(2 * p + i + 1) * H],
                                                     in0=freq[:, i * H:(i + 1) * H], scalar=0.0,
                                                     in1=phase[:, bass.ds(e * H, H)], op0=ALU.max,
                                                     op1=ALU.add).then_inc(s["relu_done"], 1)
                    if middle:
                        dve.wait_ge(s["ln_done"], T)
                        dve.wait_ge(s["relu_done"], 2 * (PAIRS * (T - 1) + p) + 2)
                        dve.scalar_tensor_tensor(out=rr[1 - par][:, cols], in0=ex[1 - par][:, cols],
                                                 scalar=float(1 / TWO_PI), in1=rr[1 - par][:, cols],
                                                 op0=ALU.mult, op1=ALU.add).then_inc(s["theta_sum"], 1)
                    if p and middle:
                        whole_turns_off(T - 1, 1 - par, p - 1)
                    if not p and last:
                        whole_turns_off(T - 2, par, PAIRS - 1)
            tiles_loop(dve, tiles)

            dve.wait_ge(s["wk_done"], 1)

            def results(g, par):
                if t_in(g, 0, NG):
                    dve.wait_ge(o12_in[par], 16 * (g - par) + 32)
                    for b in range(GRP):
                        n = g * GRP + b
                        dve.wait_ge(s["y1_done"], n + 1)
                        dve.scalar_tensor_tensor(out=batch(o1, n), in0=batch(o2, n), scalar=wk[:, bass.ds(B + n, 1)],
                                                 in1=batch(o1, n), op0=ALU.mult, op1=ALU.add).then_inc(s["y2_done"], 1)
                if t_in(g, 1, NG + 1):
                    dve.wait_ge(s["sq_done"], GRP * g)
                    dve.tensor_scalar(batch(sse, g - 1, GRP), batch(ss, g - 1, GRP),
                                      1.0 / P, RMS_EPS, ALU.mult, ALU.add).then_inc(s["rms_var"], 1)
                if t_in(g, 2, NG + 2):
                    dve.wait_ge(s["rms_done"], g - 1)
                    for b in range(GRP):
                        n = (g - 2) * GRP + b
                        dve.scalar_tensor_tensor(out=batch(o1, n), in0=batch(o1, n), scalar=rs3[:, bass.ds(n, 1)],
                                                 in1=nw[:, :], op0=ALU.mult, op1=ALU.mult).then_inc(s["yn_done"], 1)
            results_loop(dve, results)

        @block.gpsimd
        def _(pool):
            for t in kexp + vexp:
                pool.memset(t, 0.0).then_inc(s["zero_ready"], 1)
            pool.memset(halfneg[:, :], -0.5).then_inc(s["pow_ready"], 1)
            pool.wait_ge(s["pow_ready"], 1)
            pool.wait_ge(s["consts_in"], 16)

            def root(var_sem, rstd_sem, out_, in_, count):
                pool.wait_ge(var_sem, count + 1)
                pool.tensor_tensor(out_, in_, halfneg[:, 0:GRP], ALU.pow).then_inc(rstd_sem, 1)

            def rotate_k(m, g, par):
                pool.wait_ge(s["ctx_in"], 16 * g + 16)
                wait(pool, s["k_exp"], m)
                pool.tensor_tensor(k1[:, :], batch(ca, m), cst[:, C_CK:C_CK + P], ALU.mult).then_inc(s["k_mul"], 1)
                pool.tensor_tensor(k2[:, :], batch(ca, m), cst[:, C_SK:C_SK + P], ALU.mult).then_inc(s["k_mul"], 1)
                pool.wait_ge(s["k_mul"], 2 * m + 2)
                wait(pool, s["k_turned"], m - 1)
                pool.tensor_tensor(by_group_pairs(kexp[par]), group_pairs(k1[:, :]), group_pairs(k2[:, :])[:, :, :, ::-1],
                                   ALU.add).then_inc(s["k_exp"], 1)

            def scatter(R, first, last):
                if first == 0:
                    wait_apart(pool, (s["slot_done"], R + 1), (s["row_copied"], K * R + K), (s["row_id"], R + 1))
                for c in range(first, last):
                    pool.indirect_dma_start(xg, bass.IndirectOffsetOnAxis(ap=sli[:, c:c + 1], axis=0),
                                            rowb[:, c * ROW:(c + 1) * ROW], None,
                                            bounds_check=NULL_ROW - 1, oob_is_err=False).then_inc(s["rows_scattered"], 16)

            pool.wait_ge(s["zero_ready"], ZEROED)
            root(s["ln1_var"], s["ln1_rstd"], batch(rstd1, 0, GRP), ve1[:, :], 0)
            for i in range(2):
                rotate_k(i, 0, i)

            def body(G):
                for i in range(GRP):
                    n = GRP * G + i
                    if is_in(G, 0, NG) and not (isinstance(G, int) and n + 2 >= B):
                        rotate_k(n + 2, G + (i + 2) // GRP, i % 2)
                    if i == 1:
                        if is_in(G, 0, NG - 1):
                            root(s["ln1_var"], s["ln1_rstd"], batch(rstd1, G + 1, GRP), ve1[:, :], G + 1)
                        if is_in(G, 1, NG + 1):
                            root(s["ln2_var"], s["ln2_rstd"], batch(rstd2, G - 1, GRP), ve2[:, :], G - 1)
                    if is_in(G, 2, NG + 2):
                        if i == 2:
                            scatter(G - 2, 0, 4)
                        if i == 3:
                            scatter(G - 2, 4, 8)
            groups_loop(pool, body)

            def scatter_outputs(T, par, p):
                wait_apart(pool, (s["o_copied"], PAIRS * T + p + 1))
                for t in (2 * p, 2 * p + 1):
                    pool.indirect_dma_start(yg, bass.IndirectOffsetOnAxis(ap=oid[par][:, t:t + 1], axis=0),
                                            ob[:, t * P:(t + 1) * P], None,
                                            bounds_check=K * TOK - 1, oob_is_err=False).then_inc(o_scattered[p], 16)

            def tiles(T, par):
                for p in range(PAIRS):
                    if t_in(T, 1, NTG + 1):
                        m = PAIRS * (T - 1) + p
                        wait_apart(pool, (s["theta_sum"], m + 1), (s["theta_done"], m - 1))
                        pool.tensor_scalar(turn[p % 2][:, :], rr[1 - par][:, p * 2 * H:(p + 1) * 2 * H], 1.0, float(MAGIC),
                                           ALU.mult, ALU.add).then_inc(s["turns_done"], 1)
                    if p and t_in(T, 2, NTG + 2):
                        scatter_outputs(T - 2, par, p - 1)
                if t_in(T, 2, NTG + 2):
                    scatter_outputs(T - 2, par, PAIRS - 1)
                if t_in(T, 0, NTG):
                    wait_apart(pool, (xt_in[par], 64 * (T - par) + 128), *((o_scattered[p], 32 * (T - 1)) for p in range(PAIRS)))
                    pool.tensor_copy(oid[par][:, :], xt[par][:, :].rearrange("p (t w) -> p t w", w=ROW)[:, :, P].bitcast(I32)
                                     ).then_inc(s["idx_copied"], 1)
            tiles_loop(pool, tiles)

            def results(g, par):
                if t_in(g, 1, NG + 1):
                    root(s["rms_var"], s["rms_done"], batch(rs3, g - 1, GRP), batch(sse, g - 1, GRP), g - 1)
                if t_in(g, 2, NG + 2):
                    pool.wait_ge(s["yn_done"], GRP * (g - 1))
                    pool.tensor_tensor(batch(o1, g - 2, GRP * P), batch(o1, g - 2, GRP * P), batch(xa, g - 2, GRP * P),
                                       ALU.add).then_inc(s["out_ready"], 1)
            results_loop(pool, results)


_INS = ["x", "ctx_1024", "L0_ffn_router_w", "L0_ffn_router_bias", "L0_ffn_bank_mag", "L0_ffn_bank_freq",
        "L0_ffn_bank_phase", "L0_ffn_bank_down", "L0_ffn_norm_w"]


def kernel(**inputs):
    import numpy as _np
    import concourse.bacc as _bacc
    from concourse import mybir as _mybir
    from concourse.bass_utils import run_bass_kernel_spmd as _run

    nc = _bacc.Bacc("TRN2", target_bir_lowering=False, num_devices=1)
    arrays, args = {}, []
    values = [(name, _np.ascontiguousarray(inputs[name])) for name in _INS]
    values += [("consts", constants()), ("rows_of", output_rows())]
    for name, a in values:
        arrays[f"in_{name}"] = a
        args.append(nc.dram_tensor(f"in_{name}", a.shape, _mybir.dt.from_np(a.dtype), kind="ExternalInput").ap())
    args.append(nc.dram_tensor("out_0", (B, P, P), _mybir.dt.float32, kind="ExternalOutput").ap())
    build(nc, *args)
    r = _run(nc, [arrays], core_ids=[0])
    return r.results[0]["out_0"]
```

```python
from contextlib import ExitStack

import numpy as np

import concourse.bass as bass
from concourse import mybir

F32 = mybir.dt.float32
BF16 = mybir.dt.bfloat16
I32 = mybir.dt.int32
U32 = mybir.dt.uint32
ALU = mybir.AluOpType
ACT = mybir.ActivationFunctionType
AX = mybir.AxisListType

P = 128
B = 32
HEADS = 16
HEAD = P // HEADS
JH = 4
CHUNKS = 4
CHUNK = P // CHUNKS
GRP = 4
NG = B // GRP
E = 16
H = 256
K = 2
TOK = B * P
ROW = 132
REG = TOK + P
NULL_ROW = E * REG
NT = TOK * K // P + E
TG = 8
PAIRS = TG // 2
NTG = NT // TG
ZEROED = 9
DROP = 1 << 20
LN_EPS, RMS_EPS = 1e-5, 1e-6
TWO_PI = 2 * np.pi
MAGIC = 1.5 * 2.0 ** 23

C_CQ, C_SQ, C_CK, C_SK, C_CAUSAL, C_IDENT, C_BEFORE, C_ONES, C_HEAD, C_SELECT = (P * i for i in range(10))
C_IOTA = 10 * P
C_BASE = C_IOTA + E
C_TILE = C_BASE + E
C_EARLIER = C_TILE + NT
C_END = C_EARLIER + CHUNKS - 1


def constants():
    c = np.zeros((P, C_END), np.float64)
    pos = np.arange(P)[:, None]
    f = np.arange(P)[None, :]
    head, pair, odd = f // HEAD, (f % HEAD) // 2, f % 2
    gamma = 1.0 - np.exp(np.linspace(np.log(1.0 / 32.0), np.log(1.0 / 512.0), HEADS))[head]
    scale = ((2.0 * pair + 0.4 * HEAD) / (1.4 * HEAD)) ** (pos / 512.0)
    angle = pos / 10000.0 ** (pair / (HEAD // 2))
    sign = np.where(odd == 1, 1.0, -1.0)
    grow, shrink = scale * gamma ** pos, 1.0 / (scale * gamma ** pos)
    c[:, C_CQ:C_CQ + P] = np.cos(angle) * grow
    c[:, C_SQ:C_SQ + P] = np.sin(angle) * sign * grow
    c[:, C_CK:C_CK + P] = np.cos(angle) * shrink
    c[:, C_SK:C_SK + P] = (np.sin(angle) * sign * shrink)[:, np.arange(P) ^ 1]
    c[:, C_CAUSAL:C_CAUSAL + P] = f % CHUNK >= pos % CHUNK
    c[:, C_HEAD:C_HEAD + P] = pos // HEAD == head
    g, ch, d = np.arange(P) // 32, np.arange(P) // HEAD % CHUNKS, np.arange(P) % HEAD
    c[:, C_SELECT:C_SELECT + P] = ((ch[:, None] == g[None, :]) & (g[:, None] == ch[None, :]) & (d[:, None] == d[None, :]))
    c[:, C_IDENT:C_IDENT + P] = f == pos
    c[:, C_BEFORE:C_BEFORE + P] = pos < f
    c[:, C_ONES:C_ONES + P] = 1.0
    c[:, C_IOTA:C_IOTA + E] = np.arange(E)
    c[:, C_BASE:C_BASE + E] = np.arange(E) * REG
    c[:, C_TILE:C_TILE + NT] = np.arange(NT)
    c[:, C_EARLIER:C_END] = pos < CHUNK * np.arange(1, CHUNKS)
    return c.astype(np.float32)


def output_rows():
    s, b, k = np.meshgrid(np.arange(P), np.arange(B), np.arange(K), indexing="ij")
    return np.ascontiguousarray((k * TOK + b * P + s).reshape(P, B * K).astype(np.int32))


def wait(eng, sem, value):
    if not isinstance(value, int) or value > 0:
        eng.wait_ge(sem, value)


def build(nc, x, ctx_in, router_w, router_bias, bank_mag, bank_freq, bank_phase, bank_down, norm_w,
          consts, rows_of, out):
    xg = nc.dram_tensor("routed_rows", (NULL_ROW + P, ROW), F32).ap()
    yg = nc.dram_tensor("expert_outputs", (K * TOK, P), F32).ap()
    x_v = x.rearrange("b s f -> s b f")
    ctx_v = ctx_in.rearrange("b s f -> s b f")
    out_v = out.rearrange("b s f -> s b f")
    yg_v = yg.rearrange("(k b s) f -> s k b f", k=K, b=B)

    with ExitStack() as st:
        def sb(name, cols, dt=F32, parts=P):
            return st.enter_context(nc.sbuf_tensor(name, [parts, cols], dt))

        def sem(name):
            return st.enter_context(nc.semaphore(name))

        cst = sb("cst", C_END)
        rowid = sb("rowid", B * K, I32)
        wmf = sb("wmf", E * 2 * H)
        wdn = sb("wdn", E * 2 * P)
        phase = sb("phase", E * H)
        xa = sb("xa", B * P)
        ca = sb("ca", B * P)
        rw = sb("rw", P, parts=E)
        rwT = sb("rwT", E)
        rbias = sb("rbias", E)
        nw = sb("nw", P)
        before_b = sb("before_b", P, BF16)
        ones_b = sb("ones_b", P, BF16)
        halfneg = sb("halfneg", 8)
        pad = sb("pad", ROW)
        st1, mv1, ve1, rstd1, shift1 = sb("st1", GRP * 6), sb("mv1", GRP * 2), sb("ve1", GRP), sb("rstd1", B), sb("shift1", B)
        st2, mv2, ve2, rstd2, shift2 = sb("st2", GRP * 6), sb("mv2", GRP * 2), sb("ve2", GRP), sb("rstd2", B), sb("shift2", B)
        xn = [sb(f"xn{i}", P) for i in range(2)]
        q1, q2, k1, k2 = (sb(n, P) for n in ("q1", "q2", "k1", "k2"))
        turned = sb("turned", 10 * 4 * P)
        qexp, kexp, vexp, kT, qT = ([turned[:, (2 * a + i) * 4 * P:(2 * a + i + 1) * 4 * P] for i in range(2)]
                                    for a in range(5))
        qT += [sb(f"qT{i}", 4 * P)[:, :] for i in (2, 3)]
        masked = sb("masked", 2 * HEADS * P)
        sm = [masked[:, i * 4 * P:(i + 1) * 4 * P] for i in range(2)]
        before_v = [masked[:, (8 + 3 * i) * P:(11 + 3 * i) * P] for i in range(2)]
        state = [masked[:, (14 + 3 * i) * P:(17 + 3 * i) * P] for i in range(4)]
        oT = sb("oT", P)
        xln = sb("xln", GRP * P)
        xlnT = sb("xlnT", GRP * P)
        rowbs = [sb(n, GRP * K * ROW) for n in ("rowb", "last_rowb")]
        lg = sb("lg", GRP * E)
        mx8, mi8 = sb("mx8", GRP * 8), sb("mi8", GRP * 8, U32)
        ixf = sb("ixf", GRP * K)
        oh = sb("oh", GRP * K * E)
        msel = sb("msel", GRP * E, BF16)
        posb, prod, slf = sb("posb", GRP * E), sb("prod", GRP * K * E), sb("slf", GRP * K)
        slots = [sb(n, GRP * K, I32) for n in ("slots", "last_slots")]
        msum, macc = sb("msum", E), sb("macc", E)
        macc_b = sb("macc_b", E, BF16)
        v12 = sb("v12", B * K)
        ratio = sb("ratio", B)
        whole = sb("whole", B)
        eps_of = sb("eps_of", B)
        cnt, cnt_i, nt_i, ntf = sb("cnt", E), sb("cnt_i", E, I32), sb("nt_i", E, I32), sb("ntf", E)
        tend, zero16 = sb("tend", E), sb("zero16", E)
        fill_f, fill_i = sb("fill_f", E), sb("fill_i", E, I32)
        ge = sb("ge", NT * E)
        te, ts_, tb = sb("te", NT), sb("ts_", NT), sb("tb", NT)
        te_i, tb_i = sb("te_i", NT, I32), sb("tb_i", NT, I32)
        xt = [sb(f"xt{i}", TG * ROW) for i in range(2)]
        oid = [sb(f"oid{i}", TG, I32) for i in range(2)]
        xtT = [sb(f"xtT{i}", 2 * P) for i in range(2)]
        th, ex, rr = ([t[:, i * TG * H:(i + 1) * TG * H] for i in range(2)] for t in (turned, masked, ca))
        turn = [sb(f"turn{i}", 2 * H) for i in range(2)]
        hb = [sb(f"hb{i}", 2 * H) for i in range(2)]
        hT = [sb(f"hT{i}", 4 * P) for i in range(2)]
        ob = sb("ob", TG * P)
        o1, o2 = masked, ca
        ss, sse, rs3 = (sb(n, B) for n in ("ss", "sse", "rs3"))

        ps = st.enter_context(nc.psum_tensor("ps", [P, 8, 512], F32))
        SC, P_STATE = [ps[:, i, :] for i in range(2)], ps[:, 2, 0:3 * P]
        PQ, PK = ps[:, 4, :], ps[:, 5, :]
        P_OT, P_X2 = ps[:, 6, 0:P], ps[:, 6, :]
        P_O = ps[:, 7, 0:P]
        P_LG, P_POS, P_CNT = ps[:, 3, 0:GRP * E], ps[:, 3, P:P + GRP * E], ps[:, 3, 2 * P:2 * P + E]

        P_XT, P_HT, P_DOWN = [ps[:, 4, 0:2 * P], ps[:, 7, 0:2 * P]], ps[:, 5, :], ps[:, 6, 0:2 * P]

        identity = cst[:, C_IDENT:C_IDENT + P]

        names = """waited consts_in x_in ctx_in w_in freq_in freq_scaled small_in phase_in
            tables_ready pow_ready zero_ready rw_turned rw_copied
            ln1_stats ln1_mv ln1_var ln1_rstd ln1_shift ln2_stats ln2_mv ln2_var ln2_rstd ln2_shift
            xn_done q_mul q_exp k_mul k_exp q_turned k_turned q_copied k_copied v_exp v_before
            state_sum state_done
            scores_done masked_done av_done ot_copied o_turned x2_done
            xln_done xln_turned xln_copied logits_done
            lg_done max_done maxi_done ixf_done oh_done sel_done pos_done posb_done prod_done slf_done slot_done
            row_copied row_id msum_done macc_done macc_copied rows_scattered v12_done
            cnt_done tab tab_ready scores_apart ratio_done eps_done fills_done pad_ready
            phase_ready
            idx_copied xt_turned xt_copied mf_done abs_done relu_done tanh_done exp_done ln_done sin_done
            theta_sum turns_done theta_done hid_done h_turned h_copied down_done o_copied
            y_done sq_done rms_var rms_done yn_done out_ready out_done""".split()
        s = {n: sem(n) for n in names}
        xt_in = [sem(f"xt_in{i}") for i in range(2)]
        o_scattered = [sem(f"o_scattered{i}") for i in range(PAIRS)]
        o12_in = [sem(f"o12_in{i}") for i in range(2)]

        def wait_apart(eng, *counts):
            for c, v in counts:
                if not isinstance(v, int) or v > 0:
                    eng.wait_ge(c, v)
                    eng.sem_inc(s["waited"], 1)

        def diag(t, outer, dims):
            return bass.AP(tensor=t.tensor, offset=t.offset, ap=[t.ap[0], [P + outer, 4]] + dims)

        def by_head(t):
            return diag(t, HEAD, [[32, 4], [1, HEAD]])

        def by_group_pairs(t):
            return diag(t, 32, [[2, 16], [1, 2]])

        def head_view(a):
            return a.rearrange("p (g j d) -> p j g d", g=4, j=JH)

        def group_pairs(a):
            return a.rearrange("p (g i two) -> p g i two", g=4, two=2)

        def swap(a):
            return a.rearrange("p (i two) -> p i two", two=2)[:, :, ::-1]

        def pairs(a):
            return a.rearrange("p (i two) -> p i two", two=2)

        def batch(t, n, width=P):
            return t[:, bass.ds(n * width, width)]

        def groups_loop(eng, body):
            for G in range(3):
                body(G)
            with eng.Fori(3, NG - 1) as G:
                body(G)
            for G in range(NG - 1, NG + 2):
                body(G)

        def is_last(R):
            return isinstance(R, int) and R == NG - 1

        def is_in(G, lo, hi):
            return not isinstance(G, int) or lo <= G < hi

        def tiles_loop(eng, body):
            for T in range(4):
                body(T, T % 2)
            with eng.Fori(2, NTG // 2) as u:
                body(u * 2, 0)
                body(u * 2 + 1, 1)
            body(NTG, 0)
            body(NTG + 1, 1)

        def table(eng, t, T, max_val):
            _, values = nc.values_load_multi_w_load_instructions(
                t[0:1, bass.ds(T * TG, TG)], engines=[eng.engine], min_val=0, max_val=max_val,
                skip_runtime_bounds_check_because="the table is made of sums of counts, and capped where it is written")
            return values

        def results_loop(eng, body):
            body(0, 0)
            body(1, 1)
            with eng.Fori(1, NG // 2) as u:
                body(u * 2, 0)
                body(u * 2 + 1, 1)
            body(NG, 0)
            body(NG + 1, 1)

        def t_in(T, lo, hi):
            return not isinstance(T, int) or lo <= T < hi

        def fill(eng, half):
            eng.wait_ge(s["tab"], 3)
            for row in table(eng, fill_i, half, NULL_ROW - P):
                eng.dma_start(xg[bass.ds(row, P), :], pad[:, :]).then_inc(s["fills_done"], 16)

        block = st.enter_context(nc.Block())

        @block.sync
        def _(sp):
            sp.dma_start(cst[:, :], consts).then_inc(s["consts_in"], 16)
            sp.dma_start(rw[:, :], router_w).then_inc(s["small_in"], 16)
            sp.dma_start(rbias[:, :], router_bias.rearrange("(o e) -> o e", o=1).to_broadcast([P, E])).then_inc(s["small_in"], 16)
            sp.dma_start(nw[:, :], norm_w.rearrange("(o f) -> o f", o=1).to_broadcast([P, P])).then_inc(s["small_in"], 16)
            sp.dma_start(rowid[:, :], rows_of).then_inc(s["small_in"], 16)
            with sp.Fori(0, NG) as g:
                sp.dma_start(batch(xa, g, GRP * P).rearrange("p (b f) -> p b f", b=GRP),
                             x_v[:, bass.ds(g * GRP, GRP), :]).then_inc(s["x_in"], 16)
                sp.dma_start(batch(ca, g, GRP * P).rearrange("p (b f) -> p b f", b=GRP),
                             ctx_v[:, bass.ds(g * GRP, GRP), :]).then_inc(s["ctx_in"], 16)
                wait_apart(sp, (s["x_in"], 16 * g + 16), (s["ctx_in"], 16 * g + 16))
            wmf_v = wmf[:, :].rearrange("d (e m h) -> d e m h", e=E, m=2)
            sp.dma_start(wmf_v[:, :, 0, :], bank_mag.rearrange("e d h -> d e h")).then_inc(s["w_in"], 16)
            sp.dma_start(wmf_v[:, :, 1, :], bank_freq.rearrange("e d h -> d e h")).then_inc(s["freq_in"], 16)
            sp.dma_start(wdn[:, :].rearrange("p (e c d) -> p e c d", e=E, c=2),
                         bank_down.rearrange("e (c p) d -> p e c d", c=2)).then_inc(s["w_in"], 16)
            sp.dma_start(phase[:, :], bank_phase.rearrange("(o e) h -> o (e h)", o=1).to_broadcast([P, E * H])
                         ).then_inc(s["phase_in"], 16)

            sp.wait_ge(s["pad_ready"], 2)
            sp.dma_start(xg[NULL_ROW:NULL_ROW + P, :], pad[:, :]).then_inc(s["fills_done"], 16)
            fill(sp, 0)
            sp.wait_ge(s["tab_ready"], 1)
            sp.wait_ge(s["fills_done"], 16 * (E + 1))
            sp.wait_ge(s["rows_scattered"], 16 * GRP * K * NG)

            def tiles(T, par):
                if not t_in(T, 0, NTG):
                    return
                wait_apart(sp, (s["idx_copied"], T - 1), (s["xt_turned"], PAIRS * (T - 1)))
                for i, base in enumerate(table(sp, tb_i, T, NULL_ROW)):
                    sp.dma_start(xt[par][:, i * ROW:(i + 1) * ROW], xg[bass.ds(base, P), :]).then_inc(xt_in[par], 16)
            tiles_loop(sp, tiles)

            for p in range(PAIRS):
                sp.wait_ge(o_scattered[p], 32 * NTG)

            def load_outputs(g, par):
                if not t_in(g, 0, NG):
                    return
                wait_apart(sp, (o12_in[par], 16 * (g - par)))
                for k, o in enumerate((o1, o2)):
                    sp.dma_start(batch(o, g, GRP * P).rearrange("p (b f) -> p b f", b=GRP),
                                 yg_v[:, k, bass.ds(g * GRP, GRP), :]).then_inc(o12_in[par], 16)
            results_loop(sp, load_outputs)

            with sp.Fori(0, NG) as g:
                wait_apart(sp, (s["out_ready"], g + 1))
                sp.dma_start(out_v[:, bass.ds(g * GRP, GRP), :],
                             batch(o1, g, GRP * P).rearrange("p (b f) -> p b f", b=GRP)).then_inc(s["out_done"], 16)
            sp.wait_ge(s["out_done"], 16 * NG)

        @block.tensor
        def _(pe):
            pe.wait_ge(s["consts_in"], 16)
            pe.wait_ge(s["small_in"], 64)
            pe.transpose(P_LG[:, 0:E], rw[:, :], identity[0:E, 0:E]).then_inc(s["rw_turned"], 1)

            def turn_qk(m, par):
                pe.wait_ge(s["q_exp"], m + 1)
                wait(pe, s["q_copied"], m)
                for j in range(4):
                    mm = pe.transpose(PQ[:, j * P:(j + 1) * P], qexp[par][:, j * P:(j + 1) * P], identity)
                mm.then_inc(s["q_turned"], 1)
                pe.wait_ge(s["k_exp"], m + 1)
                wait(pe, s["k_copied"], m)
                for g in range(4):
                    mm = pe.transpose(PK[:, g * P:(g + 1) * P], kexp[par][:, g * P:(g + 1) * P], identity)
                mm.then_inc(s["k_turned"], 1)
                pe.wait_ge(s["v_before"], m + 1)
                wait(pe, s["state_done"], m)
                for g in range(4):
                    mm = pe.matmul(ps[32 * g:32 * g + 32, 2, 0:3 * P], kexp[par][:, g * (P + 32):g * (P + 32) + 32],
                                   before_v[par], start=True, stop=True)
                mm.then_inc(s["state_sum"], 1)

            def scores(n, i):
                par = i % 2
                pe.wait_ge(s["q_copied"], n + 1)
                pe.wait_ge(s["k_copied"], n + 1)
                wait(pe, s["masked_done"], n - 1)
                for g in range(4):
                    for c in range(CHUNKS):
                        rows = slice(c * CHUNK, (c + 1) * CHUNK)
                        mm = pe.matmul(SC[par][rows, g * P:(g + 1) * P],
                                       kT[par][:, g * P + c * CHUNK:g * P + (c + 1) * CHUNK],
                                       qT[i].rearrange("p (j s) -> p j s", j=JH)[:, :, rows], start=True, stop=True)
                mm.then_inc(s["scores_done"], 1)

            def values(n, par, turned_groups):
                pe.wait_ge(s["masked_done"], n + 1)
                pe.wait_ge(s["v_exp"], 4 * n + 4)
                wait(pe, s["ot_copied"], n)
                wait(pe, s["xln_copied"], turned_groups)
                for j in range(JH):
                    for g in range(4):
                        h = slice((4 * g + j) * 32, (4 * g + j + 1) * 32)
                        mm = pe.matmul(P_OT[32 * g:32 * g + 32, j * CHUNK:(j + 1) * CHUNK], vexp[par][:, h], sm[par][:, h],
                                       start=True, stop=True)
                mm.then_inc(s["av_done"], 1)

            def outputs(n, i):
                pe.wait_ge(s["ot_copied"], n + 1)
                pe.wait_ge(s["state_done"], n + 1)
                wait(pe, s["x2_done"], n)
                for j in range(JH):
                    for c in range(1, CHUNKS):
                        pe.matmul(head_view(P_O[c * CHUNK:(c + 1) * CHUNK, :])[:, j],
                                  qT[i][:, j * P + c * CHUNK:j * P + (c + 1) * CHUNK],
                                  head_view(state[i][:, (c - 1) * P:c * P])[:, j], start=True, stop=False)
                    for c in range(CHUNKS):
                        mm = pe.matmul(head_view(P_O[c * CHUNK:(c + 1) * CHUNK, :])[:, j], oT[:, j * CHUNK:(j + 1) * CHUNK],
                                       cst[:, C_SELECT + c * CHUNK:C_SELECT + (c + 1) * CHUNK], start=(c == 0), stop=True)
                mm.then_inc(s["o_turned"], 1)

            def turn_xln(R):
                pe.wait_ge(s["xln_done"], GRP * R + GRP)
                wait(pe, s["ot_copied"], GRP * R + 7 if not isinstance(R, int) else min(GRP * R + 7, B))
                for b in range(GRP):
                    mm = pe.transpose(P_X2[:, b * P:(b + 1) * P], xln[:, b * P:(b + 1) * P], identity)
                mm.then_inc(s["xln_turned"], 1)

            def logits(R):
                pe.wait_ge(s["xln_copied"], R + 1)
                wait(pe, s["posb_done"], R)
                for b in range(GRP):
                    mm = pe.matmul(P_LG[:, b * E:(b + 1) * E], xlnT[:, b * P:(b + 1) * P], rwT[:, :], start=True, stop=True)
                mm.then_inc(s["logits_done"], 1)

            def positions(R):
                pe.wait_ge(s["sel_done"], R + 1)
                pe.wait_ge(s["macc_copied"], R + 1)
                pe.matmul(P_POS, before_b[:, :], msel[:, :], start=True, stop=False)
                for b in range(GRP - 1):
                    pe.matmul(P_POS[:, (b + 1) * E:].rearrange("p (b e) -> p b e", e=E), ones_b[:, :],
                              msel[:, b * E:(b + 1) * E].unsqueeze(1).to_broadcast([P, GRP - 1 - b, E]), start=False, stop=False)
                pe.matmul(P_POS.rearrange("p (b e) -> p b e", e=E), ones_b[:, :],
                          macc_b[:, :].unsqueeze(1).to_broadcast([P, GRP, E]), start=False, stop=True).then_inc(s["pos_done"], 1)

            pe.wait_ge(s["rw_copied"], 1)
            turn_qk(0, 0)

            def body(G):
                for i in range(GRP):
                    n = GRP * G + i
                    if is_in(G, 0, NG):
                        scores(n, i)
                    if is_in(G, 0, NG) and not (isinstance(G, int) and n + 1 >= B):
                        turn_qk(n + 1, (i + 1) % 2)
                    if i == 2 and is_in(G, 2, NG + 2):
                        positions(G - 2)
                    if not isinstance(G, int) or 0 <= n - 2 < B:
                        outputs(n - 2, (i - 2) % 4)
                    if not isinstance(G, int) or 0 <= n - 1 < B:
                        values(n - 1, (i + 1) % 2, G - 1)
                    if i == 3 and is_in(G, 1, NG + 1):
                        turn_xln(G - 1)
                    if i == 0 and is_in(G, 2, NG + 2):
                        logits(G - 2)
            groups_loop(pe, body)

            pe.wait_ge(s["macc_copied"], NG + 1)
            pe.matmul(P_CNT, ones_b[:, :], macc_b[:, :], start=True, stop=True).then_inc(s["cnt_done"], 1)

            pe.wait_ge(s["w_in"], 32)
            pe.wait_ge(s["freq_scaled"], 1)
            pe.wait_ge(s["tab_ready"], 1)

            def turn_x(T, par, p):
                m = PAIRS * T + p
                wait(pe, s["xt_copied"], m - 1)
                for i in range(2):
                    t = 2 * p + i
                    mm = pe.transpose(P_XT[p % 2][:, i * P:(i + 1) * P], xt[par][:, t * ROW:t * ROW + P], identity)
                mm.then_inc(s["xt_turned"], 1)

            def turn_h(m, q):
                pe.wait_ge(s["hid_done"], m + 1)
                wait(pe, s["h_copied"], m)
                for c in range(4):
                    mm = pe.transpose(P_HT[:, c * P:(c + 1) * P], hb[q][:, c * P:(c + 1) * P], identity)
                mm.then_inc(s["h_turned"], 1)

            def mag_freq(m, q, experts):
                wait(pe, s["tanh_done"], m - 1)
                wait(pe, s["abs_done"], m - 1)
                wait(pe, s["relu_done"], 2 * (m - 1))
                pe.wait_ge(s["xt_copied"], m + 1)
                for i, e in enumerate(experts):
                    for c in range(2):
                        mm = pe.matmul(ps[:, 2 * q + c, i * H:(i + 1) * H], xtT[q][:, i * P:(i + 1) * P],
                                       wmf[:, bass.ds(e * (2 * H) + c * H, H)], start=True, stop=True)
                mm.then_inc(s["mf_done"], 1)

            def down(m, q, experts):
                pe.wait_ge(s["h_copied"], m + 1)
                wait(pe, s["o_copied"], m)
                for i, e in enumerate(experts):
                    for c in range(2):
                        mm = pe.matmul(P_DOWN[:, i * P:(i + 1) * P], hT[q][:, (2 * i + c) * P:(2 * i + c + 1) * P],
                                       wdn[:, bass.ds(e * (2 * P) + c * P, P)], start=(c == 0), stop=(c == 1))
                mm.then_inc(s["down_done"], 1)

            def tiles(T, par):
                first, last = t_in(T, 0, NTG), t_in(T, 2, NTG + 2)
                if first:
                    new = table(pe, te_i, T, E - 1)
                    pe.wait_ge(xt_in[par], 64 * (T - par) + 128)
                    turn_x(T, par, 0)
                for p in range(PAIRS):
                    q = p % 2
                    if first and p + 1 < PAIRS:
                        turn_x(T, par, p + 1)
                    if first:
                        mag_freq(PAIRS * T + p, q, new[2 * p:2 * p + 2])
                    if last and p == 0:
                        old = table(pe, te_i, T - 2, E - 1)
                    if last:
                        turn_h(PAIRS * (T - 2) + p, q)
                        if p:
                            down(PAIRS * (T - 2) + p - 1, 1 - q, old[2 * p - 2:2 * p])
                if last:
                    down(PAIRS * (T - 2) + PAIRS - 1, (PAIRS - 1) % 2, old[TG - 2:])
            tiles_loop(pe, tiles)

        @block.scalar
        def _(act):
            act.wait_ge(s["rw_turned"], 1)
            act.copy(rwT[:, :], P_LG[:, 0:E]).then_inc(s["rw_copied"], 1)

            def take_qk(m, i):
                par = i % 2
                act.wait_ge(s["q_turned"], m + 1)
                wait(act, s["scores_done"], m - 1)
                act.copy(qT[i][:, :], PQ).then_inc(s["q_copied"], 1)
                act.wait_ge(s["k_turned"], m + 1)
                act.copy(kT[par][:, :], PK).then_inc(s["k_copied"], 1)

            def expand_v(m, g, par):
                wait_apart(act, (s["ctx_in"], 16 * g + 16), (s["av_done"], m - 1))
                for c in range(CHUNKS):
                    rows = slice(c * CHUNK, (c + 1) * CHUNK)
                    act.copy(vexp[par][rows, :].rearrange("p (h c d) -> p h c d", c=CHUNKS, d=HEAD)[:, :, c, :],
                             batch(ca, m)[rows, :].rearrange("p (h d) -> p h d", d=HEAD)).then_inc(s["v_exp"], 1)

            def normalise_q(m, g, i):
                if i == 0:
                    act.wait_ge(s["ln1_shift"], g + 1)
                wait(act, s["q_mul"], 2 * (m - 1))
                act.activation(xn[i % 2][:, :], batch(xa, m), ACT.Identity, scale=rstd1[:, bass.ds(m, 1)],
                               bias=shift1[:, bass.ds(m, 1)]).then_inc(s["xn_done"], 1)

            def normalise(R):
                act.wait_ge(s["ln2_shift"], R + 1)
                wait(act, s["row_copied"], K * R)
                for b in range(GRP):
                    n = GRP * R + b
                    act.activation(xln[:, b * P:(b + 1) * P], batch(xa, n), ACT.Identity, scale=rstd2[:, bass.ds(n, 1)],
                                   bias=shift2[:, bass.ds(n, 1)]).then_inc(s["xln_done"], 1)

            def copy_rows(R):
                rowb = rowbs[is_last(R)]
                if not is_last(R):
                    wait(act, s["rows_scattered"], 16 * GRP * K * R)
                act.wait_ge(s["xln_done"], GRP * R + GRP)
                rows = rowb[:, :].rearrange("p (b k w) -> p b k w", b=GRP, k=K)
                for k in range(K):
                    act.copy(rows[:, :, k, 0:P], xln[:, :].rearrange("p (b f) -> p b f", b=GRP)).then_inc(s["row_copied"], 1)

            act.wait_ge(s["zero_ready"], ZEROED)
            for i in range(2):
                normalise_q(i, 0, i)
            take_qk(0, 0)
            expand_v(0, 0, 0)

            def body(G):
                for i in range(GRP):
                    n = GRP * G + i
                    more = is_in(G, 0, NG) and not (isinstance(G, int) and n + 1 >= B)
                    if is_in(G, 0, NG) and not (isinstance(G, int) and n + 2 >= B):
                        normalise_q(n + 2, G + (i + 2) // GRP, (i + 2) % GRP)
                    if more:
                        take_qk(n + 1, (i + 1) % 4)
                    if i == 0 and is_in(G, 2, NG + 2):
                        act.wait_ge(s["xln_turned"], G - 1)
                        wait(act, s["logits_done"], G - 2)
                        act.copy(xlnT[:, :], P_X2).then_inc(s["xln_copied"], 1)
                    if not isinstance(G, int) or 0 <= n - 1 < B:
                        act.wait_ge(s["av_done"], n)
                        wait(act, s["o_turned"], n - 1)
                        act.copy(oT[:, :], P_OT).then_inc(s["ot_copied"], 1)
                    if more:
                        expand_v(n + 1, G + (i + 1) // GRP, (i + 1) % 2)
                    if i == 2 and is_in(G, 2, NG + 2):
                        copy_rows(G - 2)
                    if i == 2 and is_in(G, 1, NG + 1):
                        normalise(G - 1)
            groups_loop(act, body)

            act.wait_ge(s["pad_ready"], 2)
            fill(act, 1)

            act.wait_ge(s["freq_in"], 16)
            freqs = wmf[:, :].rearrange("d (e m h) -> d e m h", e=E, m=2)[:, :, 1, :]
            act.activation(freqs, freqs, ACT.Copy, scale=float(1 / TWO_PI)).then_inc(s["freq_scaled"], 1)
            act.wait_ge(s["phase_in"], 16)
            act.activation(phase[:, :], phase[:, :], ACT.Copy, scale=float(1 / TWO_PI),
                           bias=float((0.1 + np.pi / 2) / TWO_PI)).then_inc(s["phase_ready"], 1)

            act.wait_ge(s["scores_apart"], 1)
            act.activation(ratio[:, :], ratio[:, :], ACT.Exp).then_inc(s["ratio_done"], 1)

            def sine(T, par, p):
                m = PAIRS * T + p
                cols = slice(p * 2 * H, (p + 1) * 2 * H)
                act.wait_ge(s["theta_done"], m + 1)
                act.activation(rr[par][:, cols], rr[par][:, cols], ACT.Sin, scale=float(-TWO_PI)).then_inc(s["sin_done"], 1)

            def take_outputs(T, p):
                act.wait_ge(s["down_done"], PAIRS * T + p + 1)
                wait(act, o_scattered[p], 32 * T)
                act.copy(ob[:, 2 * p * P:(2 * p + 2) * P], P_DOWN).then_inc(s["o_copied"], 1)

            def tiles(T, par):
                act.preload_act_table_set("silu_and_others")
                for p in range(PAIRS):
                    q = p % 2
                    if t_in(T, 0, NTG):
                        act.wait_ge(s["mf_done"], PAIRS * T + p + 1)
                        wait(act, s["hid_done"], PAIRS * (T - 2) + p + 1)
                        act.activation(th[par][:, p * 2 * H:(p + 1) * 2 * H], ps[:, 2 * q, :], ACT.Tanh).then_inc(s["tanh_done"], 1)
                    if t_in(T, 2, NTG + 2):
                        act.wait_ge(s["h_turned"], PAIRS * (T - 2) + p + 1)
                        wait(act, s["down_done"], PAIRS * (T - 2) + p - 1)
                        act.copy(hT[q][:, :], P_HT).then_inc(s["h_copied"], 1)
                    if p >= 2 and t_in(T, 1, NTG + 1):
                        sine(T - 1, 1 - par, p - 2)
                    if p < 2 and t_in(T, 2, NTG + 2):
                        sine(T - 2, par, p + 2)
                    if p and t_in(T, 2, NTG + 2):
                        take_outputs(T - 2, p - 1)
                if t_in(T, 0, NTG):
                    act.preload_act_table_set("natural_log_exp_and_others")
                    act.wait_ge(s["abs_done"], PAIRS * T + PAIRS)
                    act.activation(ex[par][:, :], ex[par][:, :], ACT.Exp, scale=float(-TWO_PI)).then_inc(s["exp_done"], 1)
                    act.wait_ge(s["exp_done"], T + 1)
                    act.activation(ex[par][:, :], ex[par][:, :], ACT.Ln, bias=1.0).then_inc(s["ln_done"], 1)
                if t_in(T, 2, NTG + 2):
                    take_outputs(T - 2, PAIRS - 1)
            tiles_loop(act, tiles)

            def results(g, par):
                if t_in(g, 0, NG):
                    for b in range(GRP):
                        n = g * GRP + b
                        act.wait_ge(s["y_done"], n + 1)
                        act.activation(batch(o2, n), batch(o1, n), ACT.Square,
                                       accum_out=ss[:, bass.ds(n, 1)]).then_inc(s["sq_done"], 1)
            results_loop(act, results)

        @block.vector
        def _(dve):
            for t in qexp:
                dve.memset(t[:, :], 0.0).then_inc(s["zero_ready"], 1)
            for t in rowbs:
                dve.memset(t[:, :], 0.0).then_inc(s["zero_ready"], 1)
            dve.memset(macc[:, :], 0.0).then_inc(s["macc_done"], 1)
            dve.memset(macc_b[:, :], 0.0).then_inc(s["macc_copied"], 1)
            dve.memset(zero16[:, :], 0.0).then_inc(s["zero_ready"], 1)
            dve.memset(pad[:, 0:P], 0.0).then_inc(s["pad_ready"], 1)
            dve.memset(pad[:, P:ROW].bitcast(I32), DROP).then_inc(s["pad_ready"], 1)
            dve.wait_ge(s["consts_in"], 16)
            dve.tensor_copy(before_b[:, :], cst[:, C_BEFORE:C_BEFORE + P]).then_inc(s["tables_ready"], 1)
            dve.tensor_copy(ones_b[:, :], cst[:, C_ONES:C_ONES + P]).then_inc(s["tables_ready"], 1)

            def stats(xs, stt_, mv, ve, names, count):
                for b in range(GRP):
                    dve.bn_stats(stt_[:, 6 * b:6 * b + 6], xs(b)).then_inc(s[names[0]], 1)
                for b in range(GRP):
                    wait_apart(dve, (s[names[0]], GRP * count + b + 1))
                    dve.bn_aggr(mv[:, 2 * b:2 * b + 2], stt_[:, 6 * b:6 * b + 6]).then_inc(s[names[1]], 1)
                dve.wait_ge(s[names[1]], GRP * count + GRP)
                dve.tensor_scalar(ve[:, :], mv[:, 1:2 * GRP:2], LN_EPS, None, ALU.add).then_inc(s[names[2]], 1)

            def stats1(g):
                dve.wait_ge(s["x_in"], 16 * g + 16)
                stats(lambda b: batch(xa, GRP * g + b), st1, mv1, ve1, ["ln1_stats", "ln1_mv", "ln1_var"], g)

            def shift(mv, rstd, rstd_sem, shifts, shift_sem, g):
                dve.wait_ge(rstd_sem, g + 1)
                dve.scalar_tensor_tensor(out=batch(shifts, g, GRP), in0=mv[:, 0:2 * GRP:2], scalar=-1.0,
                                         in1=batch(rstd, g, GRP), op0=ALU.mult, op1=ALU.mult).then_inc(shift_sem, 1)

            def shift_1(g):
                shift(mv1, rstd1, s["ln1_rstd"], shift1, s["ln1_shift"], g)

            def shift_2(g):
                shift(mv2, rstd2, s["ln2_rstd"], shift2, s["ln2_shift"], g)

            def rotate_q(m, i):
                wait(dve, s["q_exp"], m)
                dve.wait_ge(s["xn_done"], m + 1)
                dve.tensor_tensor(q1[:, :], xn[i % 2][:, :], cst[:, C_CQ:C_CQ + P], ALU.mult).then_inc(s["q_mul"], 1)
                dve.tensor_tensor(pairs(q2[:, :]), swap(xn[i % 2][:, :]), pairs(cst[:, C_SQ:C_SQ + P]),
                                  ALU.mult).then_inc(s["q_mul"], 1)
                dve.wait_ge(s["q_mul"], 2 * m + 2)
                wait(dve, s["q_turned"], m - 1)
                dve.tensor_tensor(by_head(qexp[i % 2]), head_view(q1[:, :]), head_view(q2[:, :]), ALU.add).then_inc(s["q_exp"], 1)

            def earlier_v(m, g, par):
                dve.wait_ge(s["ctx_in"], 16 * g + 16)
                wait(dve, s["state_sum"], m - 1)
                dve.tensor_tensor(before_v[par].rearrange("p (c f) -> p c f", f=P),
                                  batch(ca, m).unsqueeze(1).to_broadcast([P, CHUNKS - 1, P]),
                                  cst[:, C_EARLIER:C_EARLIER + CHUNKS - 1].unsqueeze(2).to_broadcast([P, CHUNKS - 1, P]),
                                  ALU.mult).then_inc(s["v_before"], 1)

            stats1(0)
            shift_1(0)
            dve.wait_ge(s["zero_ready"], ZEROED)
            for i in range(2):
                earlier_v(i, 0, i)
                rotate_q(i, i)

            def mask(n, par):
                wait(dve, s["av_done"], n - 1)
                dve.wait_ge(s["scores_done"], n + 1)
                dve.tensor_tensor(sm[par].rearrange("p (g js) -> p g js", g=4), SC[par].rearrange("p (g js) -> p g js", g=4),
                                  cst[:, C_CAUSAL:C_CAUSAL + P].unsqueeze(1).to_broadcast([P, 4, P]),
                                  ALU.mult).then_inc(s["masked_done"], 1)

            def take_state(m, i):
                dve.wait_ge(s["state_sum"], m + 1)
                dve.tensor_tensor(state[i].rearrange("p (c f) -> p c f", f=P), P_STATE.rearrange("p (c f) -> p c f", f=P),
                                  cst[:, C_HEAD:C_HEAD + P].unsqueeze(1).to_broadcast([P, CHUNKS - 1, P]),
                                  ALU.mult).then_inc(s["state_done"], 1)

            def add_attention(n):
                dve.wait_ge(s["o_turned"], n + 1)
                dve.tensor_tensor(batch(xa, n), batch(xa, n), P_O, ALU.add).then_inc(s["x2_done"], 1)

            def stats2(R):
                dve.wait_ge(s["x2_done"], GRP * R + GRP)
                stats(lambda b: batch(xa, GRP * R + b), st2, mv2, ve2, ["ln2_stats", "ln2_mv", "ln2_var"], R)

            lg3 = lg[:, :].rearrange("p (b e) -> p b e", b=GRP)
            oh4 = oh[:, :].rearrange("p (b k e) -> p b k e", b=GRP, k=K)
            msel3 = msel[:, :].rearrange("p (b e) -> p b e", b=GRP)
            posb3 = posb[:, :].rearrange("p (b e) -> p b e", b=GRP)
            mx3 = mx8[:, :].rearrange("p (b r) -> p b r", b=GRP)
            mi3 = mi8[:, :].rearrange("p (b r) -> p b r", b=GRP)
            iota = cst[:, C_IOTA:C_IOTA + E].unsqueeze(1).unsqueeze(1)
            base = cst[:, C_BASE:C_BASE + E].unsqueeze(1)

            def take_logits(R):
                dve.wait_ge(s["logits_done"], R + 1)
                dve.tensor_tensor(lg3, P_LG.rearrange("p (b e) -> p b e", b=GRP),
                                  rbias[:, :].unsqueeze(1).to_broadcast([P, GRP, E]), ALU.add).then_inc(s["lg_done"], 1)

            def choose(R):
                wait_apart(dve, (s["lg_done"], R + 1))
                for b in range(GRP):
                    dve.max(mx3[:, b, :], lg3[:, b, :]).then_inc(s["max_done"], 1)
                for b in range(GRP):
                    wait_apart(dve, (s["max_done"], GRP * R + b + 1))
                    dve.max_index(mi3[:, b, :], mx3[:, b, :], lg3[:, b, :]).then_inc(s["maxi_done"], 1)
                dve.wait_ge(s["maxi_done"], GRP * R + GRP)
                dve.tensor_copy(ixf[:, :].rearrange("p (b k) -> p b k", k=K), mi3[:, :, 0:K]).then_inc(s["ixf_done"], 1)
                dve.tensor_copy(batch(v12, R, GRP * K).rearrange("p (b k) -> p b k", k=K), mx3[:, :, 0:K]
                                ).then_inc(s["v12_done"], 1)
                dve.wait_ge(s["ixf_done"], R + 1)
                dve.tensor_tensor(oh4, iota.to_broadcast([P, GRP, K, E]),
                                  ixf[:, :].rearrange("p (b k) -> p b k", k=K).unsqueeze(3).to_broadcast([P, GRP, K, E]),
                                  ALU.is_equal).then_inc(s["oh_done"], 1)
                dve.wait_ge(s["oh_done"], R + 1)
                dve.tensor_tensor(msel3, oh4[:, :, 0, :], oh4[:, :, 1, :], ALU.add).then_inc(s["sel_done"], 1)

            def take_positions(R):
                dve.wait_ge(s["pos_done"], R + 1)
                dve.tensor_tensor(posb3, P_POS.rearrange("p (b e) -> p b e", b=GRP), base.to_broadcast([P, GRP, E]),
                                  ALU.add).then_inc(s["posb_done"], 1)

            def place(R):
                dve.tensor_reduce(msum[:, :], msel3.rearrange("p b e -> p e b"), AX.X, ALU.add).then_inc(s["msum_done"], 1)
                dve.wait_ge(s["posb_done"], R + 1)
                dve.tensor_tensor(prod[:, :].rearrange("p (b k e) -> p b k e", b=GRP, k=K), oh4,
                                  posb3.unsqueeze(2).to_broadcast([P, GRP, K, E]), ALU.mult).then_inc(s["prod_done"], 1)
                dve.wait_ge(s["msum_done"], R + 1)
                dve.wait_ge(s["macc_done"], R + 1)
                dve.tensor_tensor(macc[:, :], macc[:, :], msum[:, :], ALU.add).then_inc(s["macc_done"], 1)
                dve.wait_ge(s["prod_done"], R + 1)
                dve.tensor_reduce(slf[:, :], prod[:, :].rearrange("p (c e) -> p c e", e=E), AX.X,
                                  ALU.add).then_inc(s["slf_done"], 1)
                dve.wait_ge(s["macc_done"], R + 2)
                dve.tensor_copy(macc_b[:, :], macc[:, :]).then_inc(s["macc_copied"], 1)
                dve.wait_ge(s["slf_done"], R + 1)
                rowb = rowbs[is_last(R)]
                if not is_last(R):
                    wait(dve, s["rows_scattered"], 16 * GRP * K * R)
                dve.tensor_copy(slots[is_last(R)][:, :], slf[:, :]).then_inc(s["slot_done"], 1)
                dve.tensor_copy(rowb[:, :].rearrange("p (c w) -> p c w", w=ROW)[:, :, P].bitcast(I32),
                                batch(rowid, R, GRP * K)).then_inc(s["row_id"], 1)

            take_state(0, 0)

            def body(G):
                for i in range(GRP):
                    n = GRP * G + i
                    if is_in(G, 0, NG):
                        mask(n, i % 2)
                        if not (isinstance(G, int) and n + 2 >= B):
                            rotate_q(n + 2, i)
                            earlier_v(n + 2, G + (i + 2) // GRP, i % 2)
                        if not (isinstance(G, int) and n + 1 >= B):
                            take_state(n + 1, (i + 1) % 4)
                    if i == 1 and is_in(G, 2, NG + 2):
                        take_logits(G - 2)
                    if i == 2 and is_in(G, 2, NG + 2):
                        take_positions(G - 2)
                    if i == 2 and is_in(G, 1, NG + 1):
                        shift_2(G - 1)
                    if not isinstance(G, int) or 0 <= n - 2 < B:
                        add_attention(n - 2)
                    if i == 1:
                        if is_in(G, 0, NG - 1):
                            shift_1(G + 1)
                        if is_in(G, 2, NG + 2):
                            choose(G - 2)
                        if is_in(G, 1, NG + 1):
                            stats2(G - 1)
                    if i == 2 and is_in(G, 2, NG + 2):
                        place(G - 2)
                    if i == 0 and is_in(G, 0, NG - 1):
                        stats1(G + 1)
            groups_loop(dve, body)

            done = [0]

            def step(ins):
                done[0] += 1
                ins.then_inc(s["tab"], 1)
                dve.wait_ge(s["tab"], done[0])
            dve.wait_ge(s["cnt_done"], 1)
            step(dve.tensor_copy(cnt[:, :], P_CNT))
            step(dve.tensor_tensor(fill_f[:, :], cnt[:, :], cst[:, C_BASE:C_BASE + E], ALU.add))
            step(dve.tensor_copy(fill_i[:, :], fill_f[:, :]))
            step(dve.tensor_scalar(cnt[:, :], cnt[:, :], float(P - 1), None, ALU.add))
            step(dve.tensor_copy(cnt_i[:, :], cnt[:, :]))
            step(dve.tensor_scalar(nt_i[:, :], cnt_i[:, :], 7, None, ALU.logical_shift_right))
            step(dve.tensor_copy(ntf[:, :], nt_i[:, :]))
            step(dve.tensor_tensor_scan(tend[:, :], ntf[:, :], zero16[:, :], 0.0, ALU.add, ALU.add))
            g1 = ge[0:1, :].rearrange("o (t e) -> o t e", e=E)
            step(dve.tensor_tensor(g1, cst[0:1, C_TILE:C_TILE + NT].unsqueeze(2).to_broadcast([1, NT, E]),
                                   tend[0:1, :].unsqueeze(1).to_broadcast([1, NT, E]), ALU.is_ge))
            step(dve.tensor_reduce(te[0:1, :], g1, AX.X, ALU.add))
            step(dve.tensor_tensor(g1, g1, ntf[0:1, :].unsqueeze(1).to_broadcast([1, NT, E]), ALU.mult))
            step(dve.tensor_reduce(ts_[0:1, :], g1, AX.X, ALU.add))
            step(dve.tensor_tensor(ts_[0:1, :], cst[0:1, C_TILE:C_TILE + NT], ts_[0:1, :], ALU.subtract))
            step(dve.tensor_scalar(ts_[0:1, :], ts_[0:1, :], float(P), None, ALU.mult))
            step(dve.scalar_tensor_tensor(out=tb[0:1, :], in0=te[0:1, :], scalar=float(REG), in1=ts_[0:1, :],
                                          op0=ALU.mult, op1=ALU.add))
            step(dve.tensor_scalar(tb[0:1, :], tb[0:1, :], float(NULL_ROW), None, ALU.min))
            step(dve.tensor_copy(tb_i[0:1, :], tb[0:1, :]))
            step(dve.tensor_scalar(te[0:1, :], te[0:1, :], float(E - 1), None, ALU.min))
            dve.tensor_copy(te_i[0:1, :], te[0:1, :]).then_inc(s["tab_ready"], 1)

            v3 = v12[:, :].rearrange("p (b k) -> p b k", k=K)
            dve.wait_ge(s["v12_done"], NG)
            dve.tensor_tensor(ratio[:, :], v3[:, :, 1], v3[:, :, 0], ALU.subtract).then_inc(s["scores_apart"], 1)
            dve.wait_ge(s["ratio_done"], 1)
            step(dve.tensor_scalar(whole[:, :], ratio[:, :], 1.0, None, ALU.add))
            dve.scalar_tensor_tensor(out=eps_of[:, :], in0=whole[:, :], scalar=RMS_EPS, in1=whole[:, :],
                                     op0=ALU.mult, op1=ALU.mult).then_inc(s["eps_done"], 1)

            dve.wait_ge(s["phase_ready"], 1)
            dve.wait_ge(s["tab_ready"], 1)

            def hidden(m, par, p):
                cols = slice(p * 2 * H, (p + 1) * 2 * H)
                dve.wait_ge(s["sin_done"], m + 1)
                wait(dve, s["h_turned"], m - 1)
                dve.tensor_tensor(hb[p % 2][:, :], th[par][:, cols], rr[par][:, cols], ALU.mult).then_inc(s["hid_done"], 1)

            def whole_turns_off(T, par, p):
                cols = slice(p * 2 * H, (p + 1) * 2 * H)
                dve.wait_ge(s["turns_done"], PAIRS * T + p + 1)
                dve.scalar_tensor_tensor(out=rr[par][:, cols], in0=turn[p % 2][:, :], scalar=-float(MAGIC),
                                         in1=rr[par][:, cols], op0=ALU.add,
                                         op1=ALU.subtract).then_inc(s["theta_done"], 1)

            def take_x(m, q):
                dve.wait_ge(s["xt_turned"], m + 1)
                wait(dve, s["mf_done"], m - 1)
                dve.tensor_copy(xtT[q][:, :], P_XT[q]).then_inc(s["xt_copied"], 1)

            def tiles(T, par):
                first, middle, last = t_in(T, 0, NTG), t_in(T, 1, NTG + 1), t_in(T, 2, NTG + 2)
                if first:
                    experts = table(dve, te_i, T, E - 1)
                    take_x(PAIRS * T, 0)
                if last:
                    hidden(PAIRS * (T - 2), par, 0)
                for p in range(PAIRS):
                    q = p % 2
                    cols = slice(p * 2 * H, (p + 1) * 2 * H)
                    if first and p + 1 < PAIRS:
                        take_x(PAIRS * T + p + 1, 1 - q)
                    if last and p + 1 < PAIRS:
                        hidden(PAIRS * (T - 2) + p + 1, par, p + 1)
                    if first:
                        dve.wait_ge(s["mf_done"], PAIRS * T + p + 1)
                        freq = ps[:, 2 * q + 1, :]
                        dve.tensor_scalar(ex[par][:, cols].bitcast(I32), freq.bitcast(I32),
                                          0x7FFFFFFF, None, ALU.bitwise_and).then_inc(s["abs_done"], 1)
                        wait(dve, s["hid_done"], PAIRS * (T - 2) + p + 1)
                        for i in range(2):
                            e = experts[2 * p + i]
                            dve.scalar_tensor_tensor(out=rr[par][:, (2 * p + i) * H:(2 * p + i + 1) * H],
                                                     in0=freq[:, i * H:(i + 1) * H], scalar=0.0,
                                                     in1=phase[:, bass.ds(e * H, H)], op0=ALU.max,
                                                     op1=ALU.add).then_inc(s["relu_done"], 1)
                    if middle:
                        dve.wait_ge(s["ln_done"], T)
                        dve.wait_ge(s["relu_done"], 2 * (PAIRS * (T - 1) + p) + 2)
                        dve.scalar_tensor_tensor(out=rr[1 - par][:, cols], in0=ex[1 - par][:, cols],
                                                 scalar=float(1 / TWO_PI), in1=rr[1 - par][:, cols],
                                                 op0=ALU.mult, op1=ALU.add).then_inc(s["theta_sum"], 1)
                    if p and middle:
                        whole_turns_off(T - 1, 1 - par, p - 1)
                    if not p and last:
                        whole_turns_off(T - 2, par, PAIRS - 1)
            tiles_loop(dve, tiles)

            dve.wait_ge(s["eps_done"], 1)

            def results(g, par):
                if t_in(g, 0, NG):
                    dve.wait_ge(o12_in[par], 16 * (g - par) + 32)
                    for b in range(GRP):
                        n = g * GRP + b
                        dve.scalar_tensor_tensor(out=batch(o1, n), in0=batch(o2, n), scalar=ratio[:, bass.ds(n, 1)],
                                                 in1=batch(o1, n), op0=ALU.mult, op1=ALU.add).then_inc(s["y_done"], 1)
                if t_in(g, 1, NG + 1):
                    dve.wait_ge(s["sq_done"], GRP * g)
                    dve.scalar_tensor_tensor(out=batch(sse, g - 1, GRP), in0=batch(ss, g - 1, GRP), scalar=1.0 / P,
                                             in1=batch(eps_of, g - 1, GRP), op0=ALU.mult, op1=ALU.add).then_inc(s["rms_var"], 1)
                if t_in(g, 2, NG + 2):
                    dve.wait_ge(s["rms_done"], g - 1)
                    for b in range(GRP):
                        n = (g - 2) * GRP + b
                        dve.scalar_tensor_tensor(out=batch(o1, n), in0=batch(o1, n), scalar=rs3[:, bass.ds(n, 1)],
                                                 in1=nw[:, :], op0=ALU.mult, op1=ALU.mult).then_inc(s["yn_done"], 1)
            results_loop(dve, results)

        @block.gpsimd
        def _(pool):
            for t in kexp + vexp:
                pool.memset(t, 0.0).then_inc(s["zero_ready"], 1)
            pool.memset(halfneg[:, :], -0.5).then_inc(s["pow_ready"], 1)
            pool.wait_ge(s["pow_ready"], 1)
            pool.wait_ge(s["consts_in"], 16)

            def root(var_sem, rstd_sem, out_, in_, count):
                pool.wait_ge(var_sem, count + 1)
                pool.tensor_tensor(out_, in_, halfneg[:, 0:GRP], ALU.pow).then_inc(rstd_sem, 1)

            def rotate_k(m, g, par):
                pool.wait_ge(s["ctx_in"], 16 * g + 16)
                wait(pool, s["k_exp"], m)
                pool.tensor_tensor(k1[:, :], batch(ca, m), cst[:, C_CK:C_CK + P], ALU.mult).then_inc(s["k_mul"], 1)
                pool.tensor_tensor(k2[:, :], batch(ca, m), cst[:, C_SK:C_SK + P], ALU.mult).then_inc(s["k_mul"], 1)
                pool.wait_ge(s["k_mul"], 2 * m + 2)
                wait(pool, s["state_sum"], m - 1)
                pool.tensor_tensor(by_group_pairs(kexp[par]), group_pairs(k1[:, :]), group_pairs(k2[:, :])[:, :, :, ::-1],
                                   ALU.add).then_inc(s["k_exp"], 1)

            def scatter(R, first, last):
                if first == 0:
                    wait_apart(pool, (s["slot_done"], R + 1), (s["row_copied"], K * R + K), (s["row_id"], R + 1))
                for c in range(first, last):
                    pool.indirect_dma_start(xg, bass.IndirectOffsetOnAxis(ap=slots[is_last(R)][:, c:c + 1], axis=0),
                                            rowbs[is_last(R)][:, c * ROW:(c + 1) * ROW], None,
                                            bounds_check=NULL_ROW - 1, oob_is_err=False).then_inc(s["rows_scattered"], 16)

            pool.wait_ge(s["zero_ready"], ZEROED)
            root(s["ln1_var"], s["ln1_rstd"], batch(rstd1, 0, GRP), ve1[:, :], 0)
            for i in range(2):
                rotate_k(i, 0, i)

            def body(G):
                for i in range(GRP):
                    n = GRP * G + i
                    if is_in(G, 0, NG) and not (isinstance(G, int) and n + 2 >= B):
                        rotate_k(n + 2, G + (i + 2) // GRP, i % 2)
                    if i == 0:
                        if is_in(G, 0, NG - 1):
                            root(s["ln1_var"], s["ln1_rstd"], batch(rstd1, G + 1, GRP), ve1[:, :], G + 1)
                    if i == 1:
                        if is_in(G, 1, NG + 1):
                            root(s["ln2_var"], s["ln2_rstd"], batch(rstd2, G - 1, GRP), ve2[:, :], G - 1)
                    if i == 2 and is_in(G, 2, NG + 2):
                        scatter(G - 2, 0, 3)
                    if i == 3 and is_in(G, 2, NG + 2):
                        scatter(G - 2, 3, 6)
                        if isinstance(G, int) and G == NG + 1:
                            scatter(NG - 1, 6, 8)
                    if i == 0 and is_in(G, 3, NG + 2):
                        scatter(G - 3, 6, 8)
            groups_loop(pool, body)

            def scatter_outputs(T, par, p):
                wait_apart(pool, (s["o_copied"], PAIRS * T + p + 1))
                for t in (2 * p, 2 * p + 1):
                    pool.indirect_dma_start(yg, bass.IndirectOffsetOnAxis(ap=oid[par][:, t:t + 1], axis=0),
                                            ob[:, t * P:(t + 1) * P], None,
                                            bounds_check=K * TOK - 1, oob_is_err=False).then_inc(o_scattered[p], 16)

            def tiles(T, par):
                for p in range(PAIRS):
                    if t_in(T, 1, NTG + 1):
                        m = PAIRS * (T - 1) + p
                        wait_apart(pool, (s["theta_sum"], m + 1), (s["theta_done"], m - 1))
                        pool.tensor_scalar(turn[p % 2][:, :], rr[1 - par][:, p * 2 * H:(p + 1) * 2 * H], 1.0, float(MAGIC),
                                           ALU.mult, ALU.add).then_inc(s["turns_done"], 1)
                    if p and t_in(T, 2, NTG + 2):
                        scatter_outputs(T - 2, par, p - 1)
                if t_in(T, 2, NTG + 2):
                    scatter_outputs(T - 2, par, PAIRS - 1)
                if t_in(T, 0, NTG):
                    wait_apart(pool, (xt_in[par], 64 * (T - par) + 128), *((o_scattered[p], 32 * (T - 1)) for p in range(PAIRS)))
                    pool.tensor_copy(oid[par][:, :], xt[par][:, :].rearrange("p (t w) -> p t w", w=ROW)[:, :, P].bitcast(I32)
                                     ).then_inc(s["idx_copied"], 1)
            tiles_loop(pool, tiles)

            def results(g, par):
                if t_in(g, 1, NG + 1):
                    root(s["rms_var"], s["rms_done"], batch(rs3, g - 1, GRP), batch(sse, g - 1, GRP), g - 1)
                if t_in(g, 2, NG + 2):
                    pool.wait_ge(s["yn_done"], GRP * (g - 1))
                    pool.tensor_tensor(batch(o1, g - 2, GRP * P), batch(o1, g - 2, GRP * P), batch(xa, g - 2, GRP * P),
                                       ALU.add).then_inc(s["out_ready"], 1)
            results_loop(pool, results)


_INS = ["x", "ctx_1024", "L0_ffn_router_w", "L0_ffn_router_bias", "L0_ffn_bank_mag", "L0_ffn_bank_freq",
        "L0_ffn_bank_phase", "L0_ffn_bank_down", "L0_ffn_norm_w"]


def kernel(**inputs):
    import numpy as _np
    import concourse.bacc as _bacc
    from concourse import mybir as _mybir
    from concourse.bass_utils import run_bass_kernel_spmd as _run

    nc = _bacc.Bacc("TRN2", target_bir_lowering=False, num_devices=1)
    arrays, args = {}, []
    values = [(name, _np.ascontiguousarray(inputs[name])) for name in _INS]
    values += [("consts", constants()), ("rows_of", output_rows())]
    for name, a in values:
        arrays[f"in_{name}"] = a
        args.append(nc.dram_tensor(f"in_{name}", a.shape, _mybir.dt.from_np(a.dtype), kind="ExternalInput").ap())
    args.append(nc.dram_tensor("out_0", (B, P, P), _mybir.dt.float32, kind="ExternalOutput").ap())
    build(nc, *args)
    r = _run(nc, [arrays], core_ids=[0])
    return r.results[0]["out_0"]
```
